# Optimizing a Trainium2 kernel written in Bass

```python
import numpy as np
import jax
import jax.numpy as jnp

def _softmax(x, axis=-1):
    return jax.nn.softmax(x, axis=axis)

def _gelu(x):
    return jax.nn.gelu(x, approximate=True)

def _silu(x):
    return jax.nn.silu(x)

def _sigmoid(x):
    return jax.nn.sigmoid(x)

def _layernorm(x, axis=-1, eps=1e-05):
    m = jnp.mean(x, axis=axis, keepdims=True)
    v = jnp.var(x, axis=axis, keepdims=True)
    return (x - m) / jnp.sqrt(v + eps)

def _scatter_add(tgt, idx, src, axis=0):
    return tgt.at[idx].add(src)

def _segment_sum(src, seg, n):
    return jax.ops.segment_sum(src, seg, n)
kernel_name = 'mk_hybrid_d1_jaxref_r8_4175bf'

def setup_inputs(seed: int=0):
    np.random.seed(seed)
    _w = jnp.asarray

    def _L0_attn_a_setup():
        import math
        import jax, jax.numpy as jnp
        import numpy as np
        N_HEADS = 16
        D_EMBED = 128
        key = jax.random.key(seed)
        ks = jax.random.split(key, 5)
        b, l, d = (2, 256, D_EMBED)
        return {'x': jax.random.normal(ks[0], (b, l, d), dtype=jnp.float32), 'w_in': jax.random.normal(ks[1], (3 * d, d), dtype=jnp.float32) * 0.02, 'b_in': jax.random.normal(ks[2], (3 * d,), dtype=jnp.float32) * 0.02, 'w_out': jax.random.normal(ks[3], (d, d), dtype=jnp.float32) * 0.02, 'b_out': jax.random.normal(ks[4], (d,), dtype=jnp.float32) * 0.02}
    _L0_attn_a_in = _L0_attn_a_setup()

    def _L0_attn_b_setup():
        import jax, jax.numpy as jnp
        import numpy as np
        DT_RANK = 64
        N_STATES = 16

        def selective_scan(u, delta, A, B, C, D):
            dA = jnp.einsum('bld,dn->bldn', delta, A)
            dB_u = jnp.einsum('bld,bld,bln->bldn', delta, u, B)
            dA_shift = jnp.concatenate([dA[:, 1:], jnp.zeros_like(dA[:, :1])], axis=1)
            dA_cumsum = jnp.exp(jnp.flip(jnp.cumsum(jnp.flip(dA_shift, axis=1), axis=1), axis=1))
            xs = jnp.cumsum(dB_u * dA_cumsum, axis=1) / (dA_cumsum + 1e-12)
            y = jnp.einsum('bldn,bln->bld', xs, C)
            return y + u * D
        key = jax.random.key(seed)
        ks = jax.random.split(key, 6)
        b, l, d = (2, 128, 128)
        dt_rank, n = (DT_RANK, N_STATES)
        x = jax.random.normal(ks[0], (b, l, d), dtype=jnp.float32)
        W_x = jax.random.normal(ks[1], (d, dt_rank + 2 * n), dtype=jnp.float32) * (1.0 / np.sqrt(d))
        W_dt = jax.random.normal(ks[2], (dt_rank, d), dtype=jnp.float32) * (1.0 / np.sqrt(dt_rank))
        b_dt = jnp.zeros((d,), dtype=jnp.float32)
        A_log = jnp.log(jnp.tile(jnp.arange(1, n + 1, dtype=jnp.float32)[None, :], (d, 1)))
        D = jnp.ones((d,), dtype=jnp.float32)
        W_out = jax.random.normal(ks[3], (d, d), dtype=jnp.float32) * (1.0 / np.sqrt(d))
        b_out = jnp.zeros((d,), dtype=jnp.float32)
        return {'x': x, 'W_x': W_x, 'W_dt': W_dt, 'b_dt': b_dt, 'A_log': A_log, 'D': D, 'W_out': W_out, 'b_out': b_out}
    _L0_attn_b_in = _L0_attn_b_setup()

    def _L0_ffn_setup():
        import jax, jax.numpy as jnp
        import numpy as np
        NUM_EXPERTS = 8
        TOP_K = 2
        D_MODEL = 128
        D_FF = 512
        B, S = (2, 256)
        key = jax.random.key(seed)
        k1, k2, k3, k4 = jax.random.split(key, 4)
        scale_in = 1.0 / np.sqrt(D_MODEL)
        scale_ff = 1.0 / np.sqrt(D_FF)
        return {'hidden_states': jax.random.normal(k1, (B, S, D_MODEL), dtype=jnp.float32), 'gate_w': jax.random.normal(k2, (D_MODEL, NUM_EXPERTS), dtype=jnp.float32) * scale_in, 'w1': jax.random.normal(k3, (NUM_EXPERTS, D_MODEL, D_FF), dtype=jnp.float32) * scale_in, 'w2': jax.random.normal(k4, (NUM_EXPERTS, D_FF, D_MODEL), dtype=jnp.float32) * scale_ff}
    _L0_ffn_in = _L0_ffn_setup()
    _d = {'L0_attn_a_x': _L0_attn_a_in['x'], 'L0_attn_a_w_in': _L0_attn_a_in['w_in'], 'L0_attn_a_b_in': _L0_attn_a_in['b_in'], 'L0_attn_a_w_out': _L0_attn_a_in['w_out'], 'L0_attn_a_b_out': _L0_attn_a_in['b_out'], 'L0_attn_b_W_x': _L0_attn_b_in['W_x'], 'L0_attn_b_W_dt': _L0_attn_b_in['W_dt'], 'L0_attn_b_b_dt': _L0_attn_b_in['b_dt'], 'L0_attn_b_A_log': _L0_attn_b_in['A_log'], 'L0_attn_b_D': _L0_attn_b_in['D'], 'L0_attn_b_W_out': _L0_attn_b_in['W_out'], 'L0_attn_b_b_out': _L0_attn_b_in['b_out'], 'L0_ffn_gate_w': _L0_ffn_in['gate_w'], 'L0_ffn_w1': _L0_ffn_in['w1'], 'L0_ffn_w2': _L0_ffn_in['w2']}
    _x0 = _d['L0_attn_a_x']
    _d['L0_attn_a_x'] = jax.random.normal(jax.random.fold_in(jax.random.key(seed), 1), (16, 256, 128), dtype=_x0.dtype)
    del _x0
    return _d

def reference(L0_attn_a_x, L0_attn_a_w_in, L0_attn_a_b_in, L0_attn_a_w_out, L0_attn_a_b_out, L0_attn_b_W_x, L0_attn_b_W_dt, L0_attn_b_b_dt, L0_attn_b_A_log, L0_attn_b_D, L0_attn_b_W_out, L0_attn_b_b_out, L0_ffn_gate_w, L0_ffn_w1, L0_ffn_w2):

    def _L0_attn_a_ref(x, w_in, b_in, w_out, b_out):
        import math
        import jax, jax.numpy as jnp
        import numpy as np
        N_HEADS = 16
        D_EMBED = 128
        b, l, d = x.shape
        h = N_HEADS
        scale = 1.0 / math.sqrt(d // h)
        x_proj = (x @ w_in.T + b_in).reshape(b, l, h, -1)
        q, k, v = jnp.split(x_proj, 3, axis=-1)
        att = jnp.einsum('blhd,bmhd->blmh', q, k) * scale
        att = jax.nn.softmax(att, axis=2)
        opt = jnp.einsum('blmh,blhd->blhd', att, v).reshape(b, l, d)
        return opt @ w_out.T + b_out

    def _L0_attn_b_ref(x, W_x, W_dt, b_dt, A_log, D, W_out, b_out):
        import jax, jax.numpy as jnp
        import numpy as np
        DT_RANK = 64
        N_STATES = 16

        def selective_scan(u, delta, A, B, C, D):
            dA = jnp.einsum('bld,dn->bldn', delta, A)
            dB_u = jnp.einsum('bld,bld,bln->bldn', delta, u, B)
            dA_shift = jnp.concatenate([dA[:, 1:], jnp.zeros_like(dA[:, :1])], axis=1)
            dA_cumsum = jnp.exp(jnp.flip(jnp.cumsum(jnp.flip(dA_shift, axis=1), axis=1), axis=1))
            xs = jnp.cumsum(dB_u * dA_cumsum, axis=1) / (dA_cumsum + 1e-12)
            y = jnp.einsum('bldn,bln->bld', xs, C)
            return y + u * D
        n = A_log.shape[1]
        A = -jnp.exp(A_log)
        x_dbl = jnp.einsum('bld,de->ble', x, W_x)
        delta = x_dbl[..., :DT_RANK]
        B = x_dbl[..., DT_RANK:DT_RANK + n]
        C = x_dbl[..., DT_RANK + n:]
        delta = jax.nn.softplus(jnp.einsum('blr,rd->bld', delta, W_dt) + b_dt)
        y = selective_scan(x, delta, A, B, C, D)
        return jnp.einsum('bld,de->ble', y, W_out) + b_out

    def _L0_ffn_ref(hidden_states, gate_w, w1, w2):
        import jax, jax.numpy as jnp
        import numpy as np
        NUM_EXPERTS = 8
        TOP_K = 2
        D_MODEL = 128
        D_FF = 512
        B, S = (2, 256)
        b, s, d = hidden_states.shape
        x = hidden_states.reshape(-1, d)
        gate_logits = x @ gate_w
        top_vals, top_idx = jax.lax.top_k(gate_logits, TOP_K)
        top_w = jax.nn.softmax(top_vals.astype(jnp.float32), axis=1).astype(x.dtype)
        combine = jnp.einsum('tke,tk->te', jax.nn.one_hot(top_idx, NUM_EXPERTS, dtype=x.dtype), top_w)
        h = jax.nn.relu(jnp.einsum('td,edf->etf', x, w1))
        expert_out = jnp.einsum('etf,efd->etd', h, w2)
        final = jnp.einsum('etd,te->td', expert_out, combine)
        return final.reshape(b, s, d)
    x = L0_attn_a_x
    x = x + _L0_attn_a_ref(_layernorm(x, axis=-1), L0_attn_a_w_in, L0_attn_a_b_in, L0_attn_a_w_out, L0_attn_a_b_out)
    x = x + _L0_ffn_ref(_layernorm(x, axis=-1), L0_ffn_gate_w, L0_ffn_w1, L0_ffn_w2)
    x = x + _L0_attn_b_ref(_layernorm(x, axis=-1), L0_attn_b_W_x, L0_attn_b_W_dt, L0_attn_b_b_dt, L0_attn_b_A_log, L0_attn_b_D, L0_attn_b_W_out, L0_attn_b_b_out)
    x = x + _L0_ffn_ref(_layernorm(x, axis=-1), L0_ffn_gate_w, L0_ffn_w1, L0_ffn_w2)
    return x

_drawn_inputs = setup_inputs


def setup_inputs(seed=0):
    import zlib

    import numpy as np

    out = dict(_drawn_inputs(seed))
    spreads = {'L0_attn_b_b_dt': (0.0, 0.1), 'L0_attn_b_D': (1.0, 0.2), 'L0_attn_b_b_out': (0.0, 0.1)}
    factors = {}
    for name, (base, spread) in spreads.items():
        noise = np.random.default_rng([zlib.crc32(name.encode()), seed]).standard_normal(out[name].shape)
        drawn = base * np.exp(spread * noise) if base else spread * noise
        out[name] = jnp.asarray(drawn.astype(out[name].dtype))
    for name, factor in factors.items():
        out[name] = (out[name] * factor).astype(out[name].dtype)
    return out
```

```python
from contextlib import ExitStack

import concourse.bass as bass
from concourse import mybir

P = 128
F32 = mybir.dt.float32
BF16 = mybir.dt.bfloat16
U32 = mybir.dt.uint32
ALU = mybir.AluOpType
ACT = mybir.ActivationFunctionType
AX = mybir.AxisListType

LN_EPS = 1e-5
SCAN_EPS = 1e-12


class Progress:

    def __init__(self, sem, events):
        self.sem, self.events, self.told = sem, events, 0

    def at(self, event, b):
        return self.sem, b * len(self.events) + (self.events.index(event) + 1)

    def done(self, event):
        assert self.events[self.told % len(self.events)] == event, (event, self.events[self.told % len(self.events)])
        self.told += 1
        return self.sem, 1


def moe_hybrid_kernel(nc, x, wqT, wkT, wvT, b_qk, b_v, woT, b_o, W_x, W_dt, b_dt, A_logT, D_skip, W_out, b_out2,
                      gate_w, w1, w2, out):
    NSEQ, L, D = x.shape
    T = L // P
    H = 16
    DH = D // H
    E, _, FF = w1.shape
    FC = FF // P
    R = W_dt.shape[0]
    N = A_logT.shape[0] // D
    SCALE = float(DH) ** -0.5
    assert D == P and T == 2 and FC == 4 and E == 8 and N == 16
    HALVES = 2 * E
    NSC = 3
    ROUNDS = T * H // 2
    CHUNKS = T * N * D // 512

    x_v = x.rearrange("b (c p) d -> b p c d", p=P)
    out_v = out.rearrange("b (c p) d -> b p c d", p=P)

    ctx = ExitStack()
    with ctx:
        def sb(name, shape, dt=F32):
            return ctx.enter_context(nc.sbuf_tensor(name, shape, dt))

        def bank(name):
            return ctx.enter_context(nc.psum_tensor(name, [P, 512], F32))

        def sem(name):
            return ctx.enter_context(nc.semaphore(name))

        ident = sb("ident", [P, P])
        upto = sb("upto", [P, P])
        after = sb("after", [P, P])
        ones = sb("ones", [P, P])
        iota8 = sb("iota8", [P, E])
        tick = sb("tick", [P, 1])
        head_mask = sb("head_mask", [P, 4])
        ln_eps = sb("ln_eps", [P, 1])
        scan_eps = sb("scan_eps", [P, 1])
        wq_s = sb("wq_s", [P, P])
        wk_s = sb("wk_s", [P, P])
        wv_s = sb("wv_s", [P, P])
        bqk_s = sb("bqk_s", [P, 2])
        bv_s = sb("bv_s", [P, P])
        wo_s = sb("wo_s", [P, P])
        bo_s = sb("bo_s", [P, P])
        wx_s = sb("wx_s", [P, R + 2 * N])
        wdt_s = sb("wdt_s", [R, P])
        bdt_s = sb("bdt_s", [P, P])
        Abc = sb("Abc", [P, N * D])
        D_s = sb("D_s", [P, P])
        wout_s = sb("wout_s", [P, P])
        bout_s = sb("bout_s", [P, P])
        gate_s = sb("gate_s", [P, E])
        w1_s = sb("w1_s", [P, E, FF])
        w2_s = sb("w2_s", [P, E, FC, P])

        xin = sb("xin", [P, T, P])
        x1 = sb("x1", [P, T, P])
        x2 = sb("x2", [P, T, P])
        x3 = sb("x3", [P, T, P])
        xo = sb("xo", [P, T, P])
        a_st = sb("a_st", [P, T, 6])
        a_mv = sb("a_mv", [P, T, 2])
        a_lv = sb("a_lv", [P, T])
        a_rs = sb("a_rs", [P, T])
        a_xn = sb("a_xn", [P, T, P])
        a_xnT = sb("a_xnT", [P, L])
        q4 = sb("q4", [P, 4, L])
        kT = sb("kT", [P, L])
        v_s = sb("v_s", [P, T, P])
        nmx = sb("nmx", [P, T, H])
        Z = sb("Z", [P, T, H])
        rz = sb("rz", [P, T, H])
        attsum = sb("attsum", [P, T, H])
        probs = sb("probs", [P, NSC, 2, L], BF16)
        o_s = sb("o_s", [P, T, P])
        oT = sb("oT", [P, L])
        xb1 = sb("xb1", [P, T, P])
        s_st = sb("s_st", [P, T, 6])
        s_mv = sb("s_mv", [P, T, 2])
        s_lv = sb("s_lv", [P, T])
        s_rs = sb("s_rs", [P, T])
        u_s = sb("u_s", [P, T, P])
        uT = sb("uT", [P, L])
        dlrT = sb("dlrT", [R, L])
        bc = sb("bc", [P, T, 2 * N])
        dpre = sb("dpre", [P, T, P])
        dabs = sb("dabs", [P, T, P])
        dexp = sb("dexp", [P, T, P])
        dlog = sb("dlog", [P, T, P])
        delta = sb("delta", [P, T, P])
        du = sb("du", [P, T, P])
        Rs = sb("Rs", [P, T, P])
        Ea = sb("Ea", [P, T, N * D])
        rr = sb("rr", [P, T, N * D])
        Pb = sb("Pb", [P, T, N * D])
        y_s = sb("y_s", [P, T, P])
        uD = sb("uD", [P, T, P])
        yD = sb("yD", [P, T, P])
        yT = sb("yT", [P, L])
        xb2 = sb("xb2", [P, T, P])
        p_st = sb("p_st", [P, T, 6])
        p_mv = sb("p_mv", [P, T, 2])
        p_lv = sb("p_lv", [P, T])
        p_rs = sb("p_rs", [P, T])
        p_xn = sb("p_xn", [P, T, P])
        p_xnT = sb("p_xnT", [P, L])
        lg = sb("lg", [P, T, E])
        top = sb("top", [P, T, 8])
        topi = sb("topi", [P, T, 8], U32)
        tdiff = sb("tdiff", [P, T, 2])
        texp = sb("texp", [P, T, 2])
        tsum = sb("tsum", [P, T])
        trec = sb("trec", [P, T])
        tw = sb("tw", [P, T, 2])
        hot = sb("hot", [P, T, 2, E])
        hotw = sb("hotw", [P, T, 2, E])
        comb = sb("comb", [P, T, E])
        xs = sb("xs", [P, T, E, P])
        xsT = {1: sb("xsT1", [P, E, L]), 2: sb("xsT2", [P, E, L])}
        hbuf = sb("hbuf", [P, 2, FC, L])
        accT = sb("accT", [P, L])

        hb = [bank("h_bank0"), bank("h_bank1")]
        acc = bank("acc_bank")
        sc = [bank(f"sc_bank{n}") for n in range(NSC)]
        ma = bank("mix_bank")
        mp = bank("prep_bank")

        w_attn, w_scan, w_gate, w_w1, w_w2 = (sem(f"w_{n}") for n in ("attn", "scan", "gate", "w1", "w2"))
        c_pool, c_dve, c_act = sem("const_pool"), sem("const_dve"), sem("const_act")
        s_xin = sem("xin_loaded")
        s_out = sem("out_stored")

        rounds = range(ROUNDS)
        attn_dve = Progress(sem("attn_dve"), ["st0", "stats0", "stats1", "xn0", "xn", "q", "v"] + [f"max{r}" for r in rounds]
                            + ["rz", "attsum", "o", "x1"])
        attn_act = Progress(sem("attn_act"), ["ln", "rstd", "xnT", "k"] + [f"exp{r}" for r in rounds] + ["oT"])
        attn_pe = Progress(sem("attn_pe"), ["xnT", "qk", "v"] + [f"score{r}" for r in rounds] + ["oT", "out"])
        attn_pool = Progress(sem("attn_pool"), ["xb"])

        chunks = range(CHUNKS)
        scan_dve = Progress(sem("scan_dve"), ["st0", "stats0", "stats1", "u0", "u", "dpre", "delta", "du", "P0", "P1"]
                            + [f"X{k}" for k in chunks[:4]] + ["y0"] + [f"X{k}" for k in chunks[4:]] + ["y", "yD", "x3"])
        scan_act = Progress(sem("scan_act"), ["ln", "rstd", "uT", "dlr", "bc", "abs", "exp", "log", "R"]
                            + [f"{w}{c}{h}" for c in range(T) for w in ("E", "L", "r") for h in range(2)] + ["yT"])
        scan_pe = Progress(sem("scan_pe"), ["uT", "xdbl", "dpre", "R"] + [f"S{k}" for k in chunks] + ["yT", "out"])
        scan_pool = Progress(sem("scan_pool"), ["arg0", "arg1", "rC0", "rC1", "uD", "xb"])

        prep_dve, prep_act, prep_pe, prep_pool, exp_pe, exp_act, exp_dve, fin_pe, fin_act, fin_dve = ({} for _ in range(10))
        for ly in (1, 2):
            prep_dve[ly] = Progress(sem(f"prep{ly}_dve"), ["st0", "stats0", "stats1", "xn0", "xn", "lg", "top0", "top1", "topi",
                                                           "diff", "sum", "rec", "w", "hot", "hotw", "comb"])
            prep_act[ly] = Progress(sem(f"prep{ly}_act"), ["ln", "rstd", "xnT", "texp"] + [f"xs{r}" for r in range(E // 2)])
            prep_pe[ly] = Progress(sem(f"prep{ly}_pe"), ["xnT", "lg"] + [f"xs{r}" for r in range(E // 2)])
            prep_pool[ly] = Progress(sem(f"prep{ly}_pool"), ["xs0", "xs1"])
            exp_pe[ly] = Progress(sem(f"exp{ly}_pe"), [f"h{e}{w}" for e in range(E) for w in range(2)] + ["sum"])
            exp_act[ly] = Progress(sem(f"exp{ly}_act"), [f"h{e}" for e in range(E)])
            exp_dve[ly] = Progress(sem(f"exp{ly}_dve"), [f"h{e}" for e in range(E)])
            fin_pe[ly] = Progress(sem(f"fin{ly}_pe"), ["t"])
            fin_act[ly] = Progress(sem(f"fin{ly}_act"), ["acc"])
            fin_dve[ly] = Progress(sem(f"fin{ly}_dve"), ["x"])

        def has(b):
            return not isinstance(b, int) or 0 <= b < NSEQ

        def wait_latest(eng, *uses):
            for progress, event, b in uses:
                if has(b):
                    eng.wait_ge(*progress.at(event, b))
                    return

        def run(eng, phase1, phase2):
            def step(i):
                phase1(i)
                phase2(i)
            for i in range(4):
                step(i)
            with eng.Fori(4, NSEQ) as i:
                step(i)
            for i in range(NSEQ, NSEQ + 3):
                step(i)

        last_round = [max(r for r in rounds if r % NSC == n) for n in range(NSC)]
        last_chunk = [max(k for k in chunks if k % NSC == n) for n in range(NSC)]

        def attn_rounds(half):
            return range((half - 3) * ROUNDS // 12, min((half - 2) * ROUNDS // 12, ROUNDS))

        block = ctx.enter_context(nc.Block())

        @block.sync
        def _(sp):
            def load_x(b):
                if not isinstance(b, int) or b > 0:
                    sp.wait_ge(*attn_pool.at("xb", b - 1))
                sp.dma_start(xin[:], x_v[b]).then_inc(s_xin, 16)

            def store(b):
                sp.wait_ge(*fin_dve[2].at("x", b))
                sp.dma_start(out_v[b], xo[:]).then_inc(s_out, 16)

            load_x(0)
            for dst, src in ((wq_s, wqT), (wk_s, wkT), (wv_s, wvT), (bqk_s, b_qk), (wo_s, woT)):
                sp.dma_start(dst[:], src).then_inc(w_attn, 16)
            for dst, src in ((bv_s, b_v), (bo_s, b_o)):
                sp.dma_start(dst[:], src.partition_broadcast(P)).then_inc(w_attn, 16)
            sp.dma_start(gate_s[:], gate_w).then_inc(w_gate, 16)
            sp.dma_start(w1_s[:], w1.rearrange("e d f -> d e f")).then_inc(w_w1, 16)
            sp.dma_start(w2_s[:], w2.rearrange("e (k f) d -> f e k d", f=P)).then_inc(w_w2, 16)

            def phase1(i):
                if has(i - 3):
                    store(i - 3)

            def phase2(i):
                if not isinstance(i, int) or i + 1 < NSEQ:
                    load_x(i + 1)

            for i in range(4):
                phase1(i)
                phase2(i)
            with sp.Fori(4, NSEQ - 1) as i:
                phase1(i)
                phase2(i)
            for i in range(NSEQ - 1, NSEQ + 3):
                phase1(i)
                phase2(i)
            sp.wait_ge(s_out, 16 * NSEQ)

        W_ATTN = 16 * 7
        W_SCAN = 16 * 7

        @block.gpsimd
        def _(pool):
            for dst, src in ((wx_s, W_x), (wdt_s, W_dt), (wout_s, W_out)):
                pool.dma_start(dst[:], src).then_inc(w_scan, 16)
            for dst, src in ((bdt_s, b_dt), (Abc, A_logT), (D_s, D_skip), (bout_s, b_out2)):
                pool.dma_start(dst[:], src.partition_broadcast(P)).then_inc(w_scan, 16)
            pool.memset(ident[:], 0.0).then_inc(c_pool, 1)
            pool.memset(upto[:], 1.0).then_inc(c_pool, 1)
            pool.memset(after[:], 1.0).then_inc(c_pool, 1)
            pool.memset(ones[:], 1.0).then_inc(c_pool, 1)
            for e in range(E):
                pool.memset(iota8[:, e:e + 1], float(e)).then_inc(c_pool, 1)
            pool.memset(ln_eps[:], LN_EPS).then_inc(c_pool, 1)
            pool.memset(scan_eps[:], SCAN_EPS).then_inc(c_pool, 1)
            pool.wait_ge(c_pool, 6 + E)
            pool.affine_select(out=ident[:], in_=ident[:], compare_op=ALU.not_equal, fill=1.0, base=0,
                               pattern=[[-1, P]], channel_multiplier=1).then_inc(c_pool, 1)
            pool.affine_select(out=upto[:], in_=upto[:], compare_op=ALU.is_ge, fill=0.0, base=0,
                               pattern=[[1, P]], channel_multiplier=-1).then_inc(c_pool, 1)
            pool.affine_select(out=after[:], in_=after[:], compare_op=ALU.is_gt, fill=0.0, base=0,
                               pattern=[[-1, P]], channel_multiplier=1).then_inc(c_pool, 1)
            pool.wait_ge(w_attn, W_ATTN)
            pool.wait_ge(w_scan, W_SCAN)

            def attn_residual(b):
                pool.wait_ge(s_xin, 16 * (b + 1))
                wait_latest(pool, (attn_dve, "x1", b - 1))
                pool.wait_ge(*attn_dve.at("xn", b))
                pool.tensor_tensor(xb1[:], xin[:], bo_s[:].unsqueeze(1).broadcast_to([P, T, P]),
                                   ALU.add).then_inc(*attn_pool.done("xb"))

            def scan_exponents(b, c):
                pool.wait_ge(*scan_act.at("R", b))
                if c == 0:
                    pool.wait_ge(c_dve, 2)
                    wait_latest(pool, (scan_dve, "y", b - 1))
                pool.tensor_tensor(Ea[:, c].rearrange("p (n d) -> p n d", n=N),
                                   Rs[:, c].unsqueeze(1).broadcast_to([P, N, D]),
                                   Abc[:].rearrange("p (n d) -> p n d", n=N), ALU.mult).then_inc(*scan_pool.done(f"arg{c}"))

            def scan_times_c(b, c):
                pool.wait_ge(*scan_act.at(f"r{c}1", b))
                r = rr[:, c].rearrange("p (n d) -> p n d", n=N)
                pool.tensor_tensor(r, r, bc[:, c, N:2 * N].unsqueeze(2).broadcast_to([P, N, D]),
                                   ALU.mult).then_inc(*scan_pool.done(f"rC{c}"))

            def scan_rest(b):
                pool.wait_ge(*scan_dve.at("u", b))
                wait_latest(pool, (scan_dve, "x3", b - 1))
                pool.tensor_tensor(uD[:], u_s[:], D_s[:].unsqueeze(1).broadcast_to([P, T, P]),
                                   ALU.mult).then_inc(*scan_pool.done("uD"))
                pool.tensor_tensor(xb2[:], x2[:], bout_s[:].unsqueeze(1).broadcast_to([P, T, P]),
                                   ALU.add).then_inc(*scan_pool.done("xb"))

            def prep_scale(ly, b, c):
                pool.wait_ge(*prep_dve[ly].at("comb", b))
                if c == 0:
                    if ly == 2:
                        wait_latest(pool, (prep_pe[1], f"xs{E // 2 - 1}", b + 1), (prep_pe[2], f"xs{E // 2 - 1}", b - 1))
                    else:
                        wait_latest(pool, (prep_pe[2], f"xs{E // 2 - 1}", b - 2), (prep_pe[1], f"xs{E // 2 - 1}", b - 1))
                pool.tensor_tensor(xs[:, c], p_xn[:, c].unsqueeze(1).broadcast_to([P, E, P]),
                                   comb[:, c].unsqueeze(2).broadcast_to([P, E, P]),
                                   ALU.mult).then_inc(*prep_pool[ly].done(f"xs{c}"))

            def phase1(i):
                if has(i):
                    attn_residual(i)
                if has(i - 2):
                    prep_scale(2, i - 2, 0)
                    prep_scale(2, i - 2, 1)

            def phase2(i):
                if has(i - 1):
                    scan_exponents(i - 1, 0)
                    scan_exponents(i - 1, 1)
                if has(i):
                    prep_scale(1, i, 0)
                    prep_scale(1, i, 1)
                if has(i - 1):
                    scan_times_c(i - 1, 0)
                    scan_times_c(i - 1, 1)
                    scan_rest(i - 1)

            run(pool, phase1, phase2)

        @block.scalar
        def _(act):
            act.preload_act_table_set("natural_log_exp_and_others")
            act.wait_ge(c_pool, 6 + E + 3)
            act.wait_ge(w_scan, W_SCAN)
            act.activation(Abc[:], Abc[:], ACT.Exp).then_inc(c_act, 1)

            def rstd(progress, dve, b, mv, lv, rs):
                act.wait_ge(*dve.at("stats1", b))
                act.activation(lv[:], mv[:, :, 1], ACT.Ln, bias=ln_eps[:]).then_inc(*progress.done("ln"))
                act.wait_ge(*progress.at("ln", b))
                act.activation(rs[:], lv[:], ACT.Exp, scale=-0.5).then_inc(*progress.done("rstd"))

            def attn_xnT(b):
                act.wait_ge(*attn_pe.at("xnT", b))
                act.activation(a_xnT[:], ma[:, 0:L], ACT.Copy).then_inc(*attn_act.done("xnT"))

            def attn_k(b):
                act.wait_ge(*attn_dve.at("q", b))
                act.activation(kT[:], ma[:, L:2 * L], ACT.Identity, bias=bqk_s[:, 1:2]).then_inc(*attn_act.done("k"))

            def attn_exp(b, r):
                c, h = r // (H // 2), 2 * (r % (H // 2))
                act.wait_ge(*attn_dve.at(f"max{r}", b))
                act.activation(probs[:, r % NSC, 0], sc[r % NSC][:, 0:L], ACT.Exp, bias=nmx[:, c, h:h + 1],
                               accum_out=Z[:, c, h:h + 1])
                act.activation(probs[:, r % NSC, 1], sc[r % NSC][:, L:2 * L], ACT.Exp, bias=nmx[:, c, h + 1:h + 2],
                               accum_out=Z[:, c, h + 1:h + 2]).then_inc(*attn_act.done(f"exp{r}"))

            def attn_oT(b):
                act.wait_ge(*attn_pe.at("oT", b))
                act.activation(oT[:], ma[:, 0:L], ACT.Copy).then_inc(*attn_act.done("oT"))

            def scan_uT(b):
                act.wait_ge(*scan_pe.at("uT", b))
                act.activation(uT[:], ma[:, 0:L], ACT.Copy).then_inc(*scan_act.done("uT"))

            def scan_xdbl(b):
                act.wait_ge(*scan_pe.at("xdbl", b))
                act.activation(dlrT[:], ma[0:R, 0:L], ACT.Copy).then_inc(*scan_act.done("dlr"))
                act.activation(bc[:], ma[:, L:L + T * 2 * N].rearrange("p (c n) -> p c n", c=T),
                               ACT.Copy).then_inc(*scan_act.done("bc"))

            def scan_softplus(b):
                act.wait_ge(*scan_dve.at("dpre", b))
                act.activation(dabs[:], dpre[:], ACT.Abs).then_inc(*scan_act.done("abs"))
                act.wait_ge(*scan_act.at("abs", b))
                act.activation(dexp[:], dabs[:], ACT.Exp, scale=-1.0).then_inc(*scan_act.done("exp"))
                act.wait_ge(*scan_act.at("exp", b))
                act.activation(dlog[:], dexp[:], ACT.Ln, bias=ones[:, 0:1]).then_inc(*scan_act.done("log"))

            def scan_R(b):
                act.wait_ge(*scan_pe.at("R", b))
                act.activation(Rs[:], ma[:, 0:T * P].rearrange("p (c d) -> p c d", c=T),
                               ACT.Copy).then_inc(*scan_act.done("R"))

            def scan_exps(b, c, what):
                for h in range(2):
                    s = slice(h * N * D // 2, (h + 1) * N * D // 2)
                    if what == "E":
                        act.wait_ge(*scan_pool.at(f"arg{c}", b))
                        act.activation(Ea[:, c, s], Ea[:, c, s], ACT.Exp).then_inc(*scan_act.done(f"E{c}{h}"))
                    elif what == "L":
                        act.wait_ge(*scan_act.at(f"E{c}{h}", b))
                        if c == 0 and h == 0:
                            wait_latest(act, (scan_dve, f"X{CHUNKS - 1}", b - 1))
                        act.activation(rr[:, c, s], Ea[:, c, s], ACT.Ln, bias=scan_eps[:]).then_inc(*scan_act.done(f"L{c}{h}"))
                    else:
                        act.wait_ge(*scan_act.at(f"L{c}{h}", b))
                        act.activation(rr[:, c, s], rr[:, c, s], ACT.Exp, scale=-1.0).then_inc(*scan_act.done(f"r{c}{h}"))

            def scan_yT(b):
                act.wait_ge(*scan_pe.at("yT", b))
                act.activation(yT[:], ma[:, 0:L], ACT.Copy).then_inc(*scan_act.done("yT"))

            def prep_xnT(ly, b):
                act.wait_ge(*prep_pe[ly].at("xnT", b))
                act.activation(p_xnT[:], mp[:, 0:L], ACT.Copy).then_inc(*prep_act[ly].done("xnT"))

            def prep_texp(ly, b):
                act.wait_ge(*prep_dve[ly].at("diff", b))
                act.activation(texp[:], tdiff[:], ACT.Exp).then_inc(*prep_act[ly].done("texp"))

            def prep_xsT(ly, b, r):
                act.wait_ge(*prep_pe[ly].at(f"xs{r}", b))
                if r == 0:
                    wait_latest(act, (exp_pe[ly], f"h{E - 1}1", b - 1))
                act.activation(xsT[ly][:, 2 * r:2 * r + 2, :], mp[:].rearrange("p (e t) -> p e t", e=2),
                               ACT.Copy).then_inc(*prep_act[ly].done(f"xs{r}"))

            def fin_acc(ly, b):
                act.wait_ge(*exp_pe[ly].at("sum", b))
                act.activation(accT[:], acc[:, 0:L], ACT.Copy).then_inc(*fin_act[ly].done("acc"))

            def hidden(ly, b, e):
                act.wait_ge(*exp_pe[ly].at(f"h{e}0", b))
                act.activation(hbuf[:, e % 2, 0:2, :], hb[0][:].rearrange("p (k t) -> p k t", k=2),
                               ACT.Relu).then_inc(*exp_act[ly].done(f"h{e}"))

            def phase1(i):
                for half in range(HALVES):
                    if half == 0 and has(i - 3):
                        fin_acc(2, i - 3)
                    if half == 0 and has(i):
                        rstd(attn_act, attn_dve, i, a_mv, a_lv, a_rs)
                    if half == 0 and has(i - 2):
                        scan_yT(i - 2)
                    if half == 1 and has(i):
                        attn_xnT(i)
                    if half == 2 and has(i):
                        attn_k(i)
                    if half == 2 and has(i - 2):
                        rstd(prep_act[2], prep_dve[2], i - 2, p_mv, p_lv, p_rs)
                    if half == 4 and has(i - 2):
                        prep_xnT(2, i - 2)
                    if half == 6 and has(i - 2):
                        prep_texp(2, i - 2)
                    if 10 <= half < 14 and has(i - 2):
                        prep_xsT(2, i - 2, half - 10)
                    if half >= 3 and has(i):
                        for r in attn_rounds(half):
                            attn_exp(i, r)
                    if half % 2 == 0 and has(i - 1):
                        hidden(1, i - 1, half // 2)

            def phase2(i):
                for half in range(HALVES):
                    if half == 0 and has(i - 1):
                        fin_acc(1, i - 1)
                    if half == 0 and has(i):
                        attn_oT(i)
                    if half == 1 and has(i - 1):
                        rstd(scan_act, scan_dve, i - 1, s_mv, s_lv, s_rs)
                    if half == 2 and has(i - 1):
                        scan_uT(i - 1)
                    if half == 3 and has(i):
                        rstd(prep_act[1], prep_dve[1], i, p_mv, p_lv, p_rs)
                    if half == 3 and has(i - 1):
                        scan_xdbl(i - 1)
                    if half == 4 and has(i - 1):
                        scan_softplus(i - 1)
                    if half == 5 and has(i):
                        prep_xnT(1, i)
                    if half == 6 and has(i - 1):
                        scan_R(i - 1)
                    if half == 7 and has(i):
                        prep_texp(1, i)
                    if has(i - 1):
                        for n, (c, what) in enumerate(((0, "E"), (0, "L"), (0, "r"), (1, "E"), (1, "L"), (1, "r"))):
                            if half == 8 + n:
                                scan_exps(i - 1, c, what)
                    if 11 <= half < 15 and has(i):
                        prep_xsT(1, i, half - 11)
                    if half % 2 == 0 and has(i - 2):
                        hidden(2, i - 2, half // 2)

            run(act, phase1, phase2)

        @block.vector
        def _(dve):
            dve.wait_ge(c_pool, 6 + E + 3)
            dve.tensor_reduce(head_mask[:], ident[:].rearrange("p (g j d) -> p j g d", j=4, d=DH), AX.XY,
                              ALU.add).then_inc(c_dve, 1)
            dve.wait_ge(c_act, 1)
            dve.tensor_scalar(Abc[:], Abc[:], -1.0, None, ALU.mult).then_inc(c_dve, 1)
            dve.wait_ge(c_dve, 1)
            dve.tensor_scalar(head_mask[:], head_mask[:], SCALE, None, ALU.mult).then_inc(c_dve, 1)
            dve.wait_ge(c_dve, 3)
            dve.wait_ge(w_attn, W_ATTN)
            dve.wait_ge(w_scan, W_SCAN)

            def stats(progress, b, src, st, mv):
                dve.bn_stats(st[:, 0, :], src[:, 0, :])
                dve.bn_stats(st[:, 1, :], src[:, 1, :]).then_inc(*progress.done("st0"))
                dve.wait_ge(*progress.at("st0", b))
                dve.memset(tick[:], 0.0)
                dve.bn_aggr(mv[:, 0, :], st[:, 0, :]).then_inc(*progress.done("stats0"))
                dve.bn_aggr(mv[:, 1, :], st[:, 1, :]).then_inc(*progress.done("stats1"))

            def normalise(progress, act_progress, b, src, mv, rs, dst, events):
                dve.wait_ge(*act_progress.at("rstd", b))
                for c in range(T):
                    dve.tensor_scalar(dst[:, c, :], src[:, c, :], mv[:, c, 0:1], rs[:, c:c + 1], ALU.subtract,
                                      ALU.mult).then_inc(*progress.done(events[c]))

            def attn_stats(b):
                dve.wait_ge(s_xin, 16 * (b + 1))
                stats(attn_dve, b, xin, a_st, a_mv)

            def attn_norm(b):
                normalise(attn_dve, attn_act, b, xin, a_mv, a_rs, a_xn, ("xn0", "xn"))

            def attn_q(b):
                dve.wait_ge(*attn_pe.at("qk", b))
                for j in range(4):
                    last = dve.tensor_scalar(q4[:, j, :], ma[:, 0:L], bqk_s[:, 0:1], head_mask[:, j:j + 1], ALU.add, ALU.mult)
                last.then_inc(*attn_dve.done("q"))

            def attn_v(b):
                dve.wait_ge(*attn_pe.at("v", b))
                dve.tensor_tensor(v_s[:], ma[:, 0:T * P].rearrange("p (c d) -> p c d", c=T),
                                  bv_s[:].unsqueeze(1).broadcast_to([P, T, P]), ALU.add).then_inc(*attn_dve.done("v"))

            def attn_max(b, r):
                c, h = r // (H // 2), 2 * (r % (H // 2))
                dve.wait_ge(*attn_pe.at(f"score{r}", b))
                dve.tensor_reduce(nmx[:, c, h:h + 2], sc[r % NSC][:].rearrange("p (h m) -> p h m", h=2), AX.X, ALU.max,
                                  negate=True).then_inc(*attn_dve.done(f"max{r}"))

            def attn_out(b):
                dve.wait_ge(*attn_act.at(f"exp{ROUNDS - 1}", b))
                dve.reciprocal(rz[:], Z[:]).then_inc(*attn_dve.done("rz"))
                dve.wait_ge(*attn_dve.at("rz", b))
                dve.tensor_tensor(attsum[:], Z[:], rz[:], ALU.mult).then_inc(*attn_dve.done("attsum"))
                dve.wait_ge(*attn_dve.at("attsum", b))
                dve.tensor_tensor(o_s[:].rearrange("p c (h d) -> p (c h) d", d=DH), v_s[:].rearrange("p c (h d) -> p (c h) d", d=DH),
                                  attsum[:].rearrange("p c h -> p (c h)").unsqueeze(2).broadcast_to([P, T * H, DH]),
                                  ALU.mult).then_inc(*attn_dve.done("o"))

            def attn_add(b):
                dve.wait_ge(*attn_pe.at("out", b))
                wait_latest(dve, (fin_dve[1], "x", b - 1))
                dve.wait_ge(*attn_pool.at("xb", b))
                dve.tensor_tensor(x1[:], ma[:, 0:T * P].rearrange("p (c d) -> p c d", c=T), xb1[:],
                                  ALU.add).then_inc(*attn_dve.done("x1"))

            def scan_stats(b):
                dve.wait_ge(*fin_dve[1].at("x", b))
                stats(scan_dve, b, x2, s_st, s_mv)

            def scan_norm(b):
                normalise(scan_dve, scan_act, b, x2, s_mv, s_rs, u_s, ("u0", "u"))

            def scan_dpre(b):
                dve.wait_ge(*scan_pe.at("dpre", b))
                dve.tensor_tensor(dpre[:], ma[:, 0:T * P].rearrange("p (c d) -> p c d", c=T),
                                  bdt_s[:].unsqueeze(1).broadcast_to([P, T, P]), ALU.add).then_inc(*scan_dve.done("dpre"))

            def scan_delta(b):
                dve.wait_ge(*scan_act.at("log", b))
                dve.scalar_tensor_tensor(out=delta[:], in0=dpre[:], scalar=0.0, in1=dlog[:], op0=ALU.max,
                                         op1=ALU.add).then_inc(*scan_dve.done("delta"))
                dve.wait_ge(*scan_dve.at("delta", b))
                dve.tensor_tensor(du[:], delta[:], u_s[:], ALU.mult).then_inc(*scan_dve.done("du"))

            def scan_inputs(b, c):
                dve.wait_ge(*scan_act.at(f"E{c}1", b))
                dve.wait_ge(*scan_dve.at("du", b))
                for n in range(N):
                    s = slice(n * D, (n + 1) * D)
                    last = dve.scalar_tensor_tensor(out=Pb[:, c, s], in0=Ea[:, c, s], scalar=bc[:, c, n:n + 1],
                                                    in1=du[:, c, :], op0=ALU.mult, op1=ALU.mult)
                last.then_inc(*scan_dve.done(f"P{c}"))

            def scan_weigh(b, k):
                c, s = k // 4, slice((k % 4) * 512, (k % 4 + 1) * 512)
                dve.wait_ge(*scan_pe.at(f"S{k}", b))
                if k % 4 == 0:
                    dve.wait_ge(*scan_pool.at(f"rC{c}", b))
                dve.tensor_tensor(Ea[:, c, s], sc[k % NSC][:], rr[:, c, s], ALU.mult).then_inc(*scan_dve.done(f"X{k}"))

            def scan_y(b, c):
                dve.wait_ge(*scan_dve.at(f"X{4 * c + 3}", b))
                dve.tensor_reduce(y_s[:, c, :], Ea[:, c].rearrange("p (n d) -> p d n", n=N), AX.X,
                                  ALU.add).then_inc(*scan_dve.done("y" if c else "y0"))

            def scan_skip(b):
                dve.wait_ge(*scan_pool.at("uD", b))
                dve.wait_ge(*scan_dve.at("y", b))
                dve.tensor_tensor(yD[:], y_s[:], uD[:], ALU.add).then_inc(*scan_dve.done("yD"))

            def scan_add(b):
                dve.wait_ge(*scan_pe.at("out", b))
                wait_latest(dve, (fin_dve[2], "x", b - 1))
                dve.wait_ge(*scan_pool.at("xb", b))
                dve.tensor_tensor(x3[:], ma[:, 0:T * P].rearrange("p (c d) -> p c d", c=T), xb2[:],
                                  ALU.add).then_inc(*scan_dve.done("x3"))

            def prep_stats(ly, b):
                src = x1 if ly == 1 else x3
                dve.wait_ge(*(attn_dve.at("x1", b) if ly == 1 else scan_dve.at("x3", b)))
                stats(prep_dve[ly], b, src, p_st, p_mv)

            def prep_norm(ly, b):
                src = x1 if ly == 1 else x3
                if ly == 2:
                    wait_latest(dve, (prep_pool[1], "xs1", b + 1), (prep_pool[2], "xs1", b - 1))
                else:
                    wait_latest(dve, (prep_pool[2], "xs1", b - 2), (prep_pool[1], "xs1", b - 1))
                normalise(prep_dve[ly], prep_act[ly], b, src, p_mv, p_rs, p_xn, ("xn0", "xn"))

            def prep_top(ly, b):
                pr = prep_dve[ly]
                dve.wait_ge(*prep_pe[ly].at("lg", b))
                dve.tensor_copy(lg[:], mp[:, L:L + T * E].rearrange("p (c e) -> p c e", c=T)).then_inc(*pr.done("lg"))
                dve.wait_ge(*pr.at("lg", b))
                dve.memset(tick[:], 0.0)
                dve.max(top[:, 0, :], lg[:, 0, :]).then_inc(*pr.done("top0"))
                dve.max(top[:, 1, :], lg[:, 1, :]).then_inc(*pr.done("top1"))
                dve.wait_ge(*pr.at("top1", b))
                dve.memset(tick[:], 0.0)
                dve.max_index(topi[:, 0, :], top[:, 0, :], lg[:, 0, :])
                dve.max_index(topi[:, 1, :], top[:, 1, :], lg[:, 1, :]).then_inc(*pr.done("topi"))
                dve.tensor_tensor(tdiff[:], top[:, :, 0:2], top[:, :, 0:1].broadcast_to([P, T, 2]),
                                  ALU.subtract).then_inc(*pr.done("diff"))

            def prep_weights(ly, b):
                pr = prep_dve[ly]
                dve.wait_ge(*prep_act[ly].at("texp", b))
                dve.tensor_reduce(tsum[:], texp[:], AX.X, ALU.add).then_inc(*pr.done("sum"))
                dve.wait_ge(*pr.at("sum", b))
                dve.reciprocal(trec[:], tsum[:]).then_inc(*pr.done("rec"))
                dve.wait_ge(*pr.at("rec", b))
                dve.tensor_tensor(tw[:], texp[:], trec[:].unsqueeze(2).broadcast_to([P, T, 2]), ALU.mult).then_inc(*pr.done("w"))
                for c in range(T):
                    last = dve.tensor_tensor(hot[:, c], topi[:, c, 0:2].unsqueeze(2).broadcast_to([P, 2, E]),
                                             iota8[:].unsqueeze(1).broadcast_to([P, 2, E]), ALU.is_equal)
                last.then_inc(*pr.done("hot"))
                dve.wait_ge(*pr.at("hot", b))
                dve.tensor_tensor(hotw[:].rearrange("p c k e -> p (c k) e"), hot[:].rearrange("p c k e -> p (c k) e"),
                                  tw[:].rearrange("p c k -> p (c k)").unsqueeze(2).broadcast_to([P, 2 * T, E]),
                                  ALU.mult).then_inc(*pr.done("hotw"))
                dve.wait_ge(*pr.at("hotw", b))
                dve.tensor_tensor(comb[:], hotw[:, :, 0, :], hotw[:, :, 1, :], ALU.add).then_inc(*pr.done("comb"))

            def fin_add(ly, b):
                dve.wait_ge(*fin_pe[ly].at("t", b))
                src, dst = (x1, x2) if ly == 1 else (x3, xo)
                if ly == 1:
                    wait_latest(dve, (scan_pool, "xb", b - 1))
                elif not isinstance(b, int) or b > 0:
                    dve.wait_ge(s_out, 16 * b)
                dve.tensor_tensor(dst[:], mp[:, 0:T * P].rearrange("p (c d) -> p c d", c=T), src[:],
                                  ALU.add).then_inc(*fin_dve[ly].done("x"))

            def hidden(ly, b, e):
                dve.wait_ge(*exp_pe[ly].at(f"h{e}1", b))
                dve.tensor_scalar(hbuf[:, e % 2, 2:4, :], hb[1][:].rearrange("p (k t) -> p k t", k=2), 0.0, None,
                                  ALU.max).then_inc(*exp_dve[ly].done(f"h{e}"))

            def phase1(i):
                for half in range(HALVES):
                    if half == 0:
                        if has(i):
                            attn_stats(i)
                        if has(i - 2):
                            scan_skip(i - 2)
                        if has(i):
                            attn_norm(i)
                        if has(i - 3):
                            fin_add(2, i - 3)
                    if half == 1:
                        if has(i - 2):
                            scan_add(i - 2)
                            prep_stats(2, i - 2)
                    if half == 2 and has(i):
                        attn_q(i)
                    if half == 3:
                        if has(i):
                            attn_v(i)
                        if has(i - 2):
                            prep_norm(2, i - 2)
                    if half == 5 and has(i - 2):
                        prep_top(2, i - 2)
                    if half == 7 and has(i - 2):
                        prep_weights(2, i - 2)
                    if half >= 3 and has(i):
                        for r in attn_rounds(half):
                            attn_max(i, r)
                    if half % 2 == 1 and has(i - 1):
                        hidden(1, i - 1, half // 2)

            def phase2(i):
                for half in range(HALVES):
                    if half == 0:
                        if has(i):
                            attn_out(i)
                        if has(i - 1):
                            fin_add(1, i - 1)
                            scan_stats(i - 1)
                    if half == 1:
                        if has(i - 1):
                            scan_norm(i - 1)
                        if has(i):
                            attn_add(i)
                            prep_stats(1, i)
                    if half == 3 and has(i):
                        prep_norm(1, i)
                    if half == 4 and has(i - 1):
                        scan_dpre(i - 1)
                    if half == 5 and has(i - 1):
                        scan_delta(i - 1)
                    if half == 6 and has(i):
                        prep_top(1, i)
                    if half == 8 and has(i):
                        prep_weights(1, i)
                    if half == 9 and has(i - 1):
                        scan_inputs(i - 1, 0)
                    if half == 12 and has(i - 1):
                        scan_inputs(i - 1, 1)
                    if half % 2 == 1 and has(i - 2):
                        hidden(2, i - 2, half // 2)
                    if half >= 14 and has(i - 1):
                        c = half - 14
                        for k in range(4 * c, 4 * c + 4):
                            scan_weigh(i - 1, k)
                        scan_y(i - 1, c)

            run(dve, phase1, phase2)

        @block.tensor
        def _(pe):
            pe.wait_ge(c_pool, 6 + E + 3)
            pe.wait_ge(w_attn, W_ATTN)
            pe.wait_ge(w_scan, W_SCAN)
            pe.wait_ge(w_gate, 16)

            def transposes(dst, src, progress, event):
                for c in range(T):
                    last = pe.transpose(dst[:, c * P:(c + 1) * P], src[:, c, :], ident[:])
                last.then_inc(*progress.done(event))

            def token_products(dst, srcT, w, progress, event):
                for c in range(T):
                    last = pe.matmul(dst[:, c * P:(c + 1) * P], srcT[:, c * P:(c + 1) * P], w[:], start=True, stop=True)
                last.then_inc(*progress.done(event))

            def attn_xnT(b):
                wait_latest(pe, (scan_dve, "x3", b - 2), (attn_dve, "x1", b - 1))
                pe.wait_ge(*attn_dve.at("xn", b))
                transposes(ma, a_xn, attn_pe, "xnT")

            def attn_qk(b):
                pe.wait_ge(*attn_act.at("xnT", b))
                pe.matmul(ma[:, 0:L], wq_s[:], a_xnT[:], start=True, stop=True)
                pe.matmul(ma[:, L:2 * L], wk_s[:], a_xnT[:], start=True, stop=True).then_inc(*attn_pe.done("qk"))

            def attn_v(b):
                pe.wait_ge(*attn_act.at("k", b))
                token_products(ma, a_xnT, wv_s, attn_pe, "v")

            def attn_score(b, r):
                c, h = r // (H // 2), 2 * (r % (H // 2))
                if r == 0:
                    pe.wait_ge(*attn_act.at("k", b))
                if r >= NSC:
                    pe.wait_ge(*attn_act.at(f"exp{r - NSC}", b))
                else:
                    wait_latest(pe, (scan_dve, f"X{last_chunk[r]}", b - 2), (attn_act, f"exp{last_round[r]}", b - 1))
                g = slice(32 * (h // 4), 32 * (h // 4) + 32)
                for n in range(2):
                    last = pe.matmul(sc[r % NSC][:, n * L:(n + 1) * L], q4[g, h % 4 + n, c * P:(c + 1) * P], kT[g, :],
                                     start=True, stop=True)
                last.then_inc(*attn_pe.done(f"score{r}"))

            def attn_oT(b):
                pe.wait_ge(*attn_dve.at("v", b))
                pe.wait_ge(*attn_dve.at("o", b))
                transposes(ma, o_s, attn_pe, "oT")

            def attn_proj(b):
                pe.wait_ge(*attn_act.at("oT", b))
                token_products(ma, oT, wo_s, attn_pe, "out")

            def scan_uT(b):
                wait_latest(pe, (attn_dve, "x1", b + 1), (scan_dve, "x3", b - 1))
                pe.wait_ge(*scan_dve.at("u", b))
                transposes(ma, u_s, scan_pe, "uT")

            def scan_xdbl(b):
                pe.wait_ge(*scan_act.at("uT", b))
                pe.matmul(ma[0:R, 0:L], wx_s[:, 0:R], uT[:], start=True, stop=True)
                for c in range(T):
                    o = L + c * 2 * N
                    last = pe.matmul(ma[:, o:o + 2 * N], uT[:, c * P:(c + 1) * P], wx_s[:, R:R + 2 * N], start=True, stop=True)
                last.then_inc(*scan_pe.done("xdbl"))

            def scan_dpre(b):
                pe.wait_ge(*scan_act.at("bc", b))
                token_products(ma, dlrT, wdt_s, scan_pe, "dpre")

            def scan_R(b):
                pe.wait_ge(*scan_dve.at("delta", b))
                pe.matmul(ma[:, 0:P], after[:], delta[:, 0, :], start=True, stop=False)
                pe.matmul(ma[:, 0:P], ones[:], delta[:, 1, :], start=False, stop=True)
                pe.matmul(ma[:, P:2 * P], after[:], delta[:, 1, :], start=True, stop=True).then_inc(*scan_pe.done("R"))

            def scan_sums(b, k):
                c, s = k // 4, slice((k % 4) * 512, (k % 4 + 1) * 512)
                if k % 4 == 0:
                    pe.wait_ge(*scan_dve.at(f"P{c}", b))
                if k >= NSC:
                    pe.wait_ge(*scan_dve.at(f"X{k - NSC}", b))
                else:
                    wait_latest(pe, (attn_act, f"exp{last_round[k]}", b + 1), (scan_dve, f"X{last_chunk[k]}", b - 1))
                if c == 1:
                    pe.matmul(sc[k % NSC][:], ones[:], Pb[:, 0, s], start=True, stop=False)
                pe.matmul(sc[k % NSC][:], upto[:], Pb[:, c, s], start=(c == 0), stop=True).then_inc(*scan_pe.done(f"S{k}"))

            def scan_yT(b):
                pe.wait_ge(*scan_act.at("R", b))
                pe.wait_ge(*scan_dve.at("yD", b))
                transposes(ma, yD, scan_pe, "yT")

            def scan_proj(b):
                pe.wait_ge(*scan_act.at("yT", b))
                token_products(ma, yT, wout_s, scan_pe, "out")

            def prep_xnT(ly, b):
                last_xs = f"xs{E // 2 - 1}"
                if ly == 2:
                    wait_latest(pe, (fin_dve[2], "x", b - 1), (prep_act[1], last_xs, b + 1))
                else:
                    wait_latest(pe, (fin_dve[1], "x", b - 1), (prep_act[2], last_xs, b - 2), (prep_act[1], last_xs, b - 1))
                pe.wait_ge(*prep_dve[ly].at("xn", b))
                transposes(mp, p_xn, prep_pe[ly], "xnT")

            def prep_logits(ly, b):
                pe.wait_ge(*prep_act[ly].at("xnT", b))
                for c in range(T):
                    last = pe.matmul(mp[:, L + c * E:L + (c + 1) * E], p_xnT[:, c * P:(c + 1) * P], gate_s[:], start=True, stop=True)
                last.then_inc(*prep_pe[ly].done("lg"))

            def prep_xsT(ly, b, r):
                if r == 0:
                    pe.wait_ge(*prep_dve[ly].at("lg", b))
                    pe.wait_ge(*prep_pool[ly].at("xs1", b))
                else:
                    pe.wait_ge(*prep_act[ly].at(f"xs{r - 1}", b))
                for e in range(2):
                    for c in range(T):
                        o = (e * T + c) * P
                        last = pe.transpose(mp[:, o:o + P], xs[:, c, 2 * r + e, :], ident[:])
                last.then_inc(*prep_pe[ly].done(f"xs{r}"))

            def fin_t(ly, b):
                last_xs = f"xs{E // 2 - 1}"
                if ly == 2:
                    wait_latest(pe, (prep_act[1], last_xs, b + 2), (fin_dve[1], "x", b + 1), (prep_act[2], last_xs, b))
                else:
                    wait_latest(pe, (prep_act[2], last_xs, b - 1), (prep_act[1], last_xs, b))
                pe.wait_ge(*fin_act[ly].at("acc", b))
                for c in range(T):
                    last = pe.transpose(mp[:, c * P:(c + 1) * P], accT[:, c * P:(c + 1) * P], ident[:])
                last.then_inc(*fin_pe[ly].done("t"))

            def previous_pass(ly, b):
                return ((2, b - 2), (1, b - 1)) if ly == 1 else ((1, b + 1), (2, b - 1))

            def expert_up(ly, b, e):
                if e == 0:
                    pe.wait_ge(*prep_act[ly].at(f"xs{E // 2 - 1}", b))
                for w, ready in ((0, exp_act), (1, exp_dve)):
                    if e:
                        pe.wait_ge(*ready[ly].at(f"h{e - 1}", b))
                    else:
                        wait_latest(pe, *((ready[l], f"h{E - 1}", n) for l, n in previous_pass(ly, b)))
                    for k in range(2):
                        f = (2 * w + k) * P
                        last = pe.matmul(hb[w][:, k * L:(k + 1) * L], w1_s[:, e, f:f + P], xsT[ly][:, e, :], start=True, stop=True)
                    last.then_inc(*exp_pe[ly].done(f"h{e}{w}"))

            def expert_down(ly, b, e):
                if e == 0:
                    wait_latest(pe, *((fin_act[l], "acc", n) for l, n in previous_pass(ly, b)))
                for k in range(FC):
                    if k == 0:
                        pe.wait_ge(*exp_act[ly].at(f"h{e}", b))
                    if k == 2:
                        pe.wait_ge(*exp_dve[ly].at(f"h{e}", b))
                    last = pe.matmul(acc[:, 0:L], w2_s[:, e, k, :], hbuf[:, e % 2, k, :], start=(e == 0 and k == 0),
                                     stop=(e == E - 1 and k == FC - 1))
                if e == E - 1:
                    last.then_inc(*exp_pe[ly].done("sum"))

            def experts(ly, b, half):
                if half % 2 == 0:
                    expert_up(ly, b, half // 2)
                elif half > 1:
                    expert_down(ly, b, half // 2 - 1)

            def phase1(i):
                if isinstance(i, int) and i == 1:
                    pe.wait_ge(w_w1, 16)
                    pe.wait_ge(w_w2, 16)
                for half in range(HALVES):
                    if half == 0:
                        if has(i - 2):
                            scan_yT(i - 2)
                    if half == 1:
                        if has(i - 3):
                            fin_t(2, i - 3)
                        if has(i - 2):
                            scan_proj(i - 2)
                        if has(i):
                            attn_xnT(i)
                    if half == 2 and has(i):
                        attn_qk(i)
                    if half == 3 and has(i):
                        attn_v(i)
                    if half == 4 and has(i - 2):
                        prep_xnT(2, i - 2)
                    if half == 5 and has(i - 2):
                        prep_logits(2, i - 2)
                    if 10 <= half < 14 and has(i - 2):
                        prep_xsT(2, i - 2, half - 10)
                    if half >= 3 and has(i):
                        for r in attn_rounds(half):
                            attn_score(i, r)
                    if has(i - 1):
                        experts(1, i - 1, half)
                if has(i - 1):
                    expert_down(1, i - 1, E - 1)

            def phase2(i):
                for half in range(HALVES):
                    if half == 1:
                        if has(i - 1):
                            fin_t(1, i - 1)
                        if has(i):
                            attn_oT(i)
                    if half == 2:
                        if has(i):
                            attn_proj(i)
                        if has(i - 1):
                            scan_uT(i - 1)
                    if half == 3 and has(i - 1):
                        scan_xdbl(i - 1)
                    if half == 4 and has(i - 1):
                        scan_dpre(i - 1)
                    if half == 4 and has(i):
                        prep_xnT(1, i)
                    if half == 6 and has(i):
                        prep_logits(1, i)
                    if half == 6 and has(i - 1):
                        scan_R(i - 1)
                    if 11 <= half < 15 and has(i):
                        prep_xsT(1, i, half - 11)
                    if has(i - 2):
                        experts(2, i - 2, half)
                    if half in (14, 15) and has(i - 1):
                        for k in range(4 * (half - 14), 4 * (half - 14) + 4):
                            scan_sums(i - 1, k)
                if has(i - 2):
                    expert_down(2, i - 2, E - 1)

            run(pe, phase1, phase2)


_DRAM = ["x", "wqT", "wkT", "wvT", "b_qk", "b_v", "woT", "b_o", "W_x", "W_dt", "b_dt", "A_logT", "D", "W_out", "b_out",
         "gate_w", "w1", "w2"]


def kernel(**inputs):
    import numpy as _np
    import concourse.bacc as _bacc
    from concourse import mybir as _mybir
    from concourse.bass_utils import run_bass_kernel_spmd as _run

    a = {k: _np.asarray(v) for k, v in inputs.items()}
    D = a["L0_attn_a_x"].shape[-1]
    H = 16
    w_in = a["L0_attn_a_w_in"].reshape(H, 3, D // H, D)
    b_in = a["L0_attn_a_b_in"].reshape(H, 3, D // H)
    host = {
        "x": a["L0_attn_a_x"],
        "wqT": w_in[:, 0].reshape(D, D).T, "wkT": w_in[:, 1].reshape(D, D).T, "wvT": w_in[:, 2].reshape(D, D).T,
        "b_qk": b_in[:, 0:2].transpose(0, 2, 1).reshape(D, 2), "b_v": b_in[:, 2].reshape(D),
        "woT": a["L0_attn_a_w_out"].T, "b_o": a["L0_attn_a_b_out"],
        "W_x": a["L0_attn_b_W_x"], "W_dt": a["L0_attn_b_W_dt"], "b_dt": a["L0_attn_b_b_dt"],
        "A_logT": a["L0_attn_b_A_log"].T.reshape(-1), "D": a["L0_attn_b_D"],
        "W_out": a["L0_attn_b_W_out"], "b_out": a["L0_attn_b_b_out"],
        "gate_w": a["L0_ffn_gate_w"], "w1": a["L0_ffn_w1"], "w2": a["L0_ffn_w2"],
    }
    nc = _bacc.Bacc("TRN2", target_bir_lowering=False, num_devices=1)
    arrays, args = {}, []
    for name in _DRAM:
        v = _np.ascontiguousarray(host[name])
        arrays[f"in_{name}"] = v
        args.append(nc.dram_tensor(f"in_{name}", v.shape, _mybir.dt.from_np(v.dtype), kind="ExternalInput").ap())
    shape = a["L0_attn_a_x"].shape
    args.append(nc.dram_tensor("out_0", shape, F32, kind="ExternalOutput").ap())
    moe_hybrid_kernel(nc, *args)
    r = _run(nc, [arrays], core_ids=[0])
    return r.results[0]["out_0"]
```

```python
from contextlib import ExitStack

import concourse.bass as bass
from concourse import mybir

P = 128
F32 = mybir.dt.float32
BF16 = mybir.dt.bfloat16
F32R = mybir.dt.float32r
U32 = mybir.dt.uint32
ALU = mybir.AluOpType
ACT = mybir.ActivationFunctionType
AX = mybir.AxisListType

LN_EPS = 1e-5
SCAN_EPS = 1e-12


class Progress:

    def __init__(self, sem, events):
        self.sem, self.events, self.told = sem, events, 0

    def at(self, event, b):
        return self.sem, b * len(self.events) + (self.events.index(event) + 1)

    def done(self, event):
        assert self.events[self.told % len(self.events)] == event, (event, self.events[self.told % len(self.events)])
        self.told += 1
        return self.sem, 1


def moe_hybrid_kernel(nc, x, wqkT, wvT, b_qk, b_v, woT, b_o, W_x, W_dt, b_dt, A_logT, D_skip, W_out, b_out2,
                      gate_w, w1, w2, out):
    NSEQ, L, D = x.shape
    T = L // P
    H = 16
    DH = D // H
    E, _, FF = w1.shape
    FC = FF // P
    R = W_dt.shape[0]
    N = A_logT.shape[0] // D
    SCALE = float(DH) ** -0.5
    assert D == P and T == 2 and FC == 4 and E == 8 and N == 16
    HALVES = 2 * E
    NSC = 3
    ROUNDS = H
    HG = 4
    LOW_COPY = (2, 1)
    CHUNKS = T * N * D // 512

    x_v = x.rearrange("b (c p) d -> b p c d", p=P)
    out_v = out.rearrange("b (c p) d -> b p c d", p=P)

    ctx = ExitStack()
    with ctx:
        def sb(name, shape, dt=F32):
            return ctx.enter_context(nc.sbuf_tensor(name, shape, dt))

        def bank(name):
            return ctx.enter_context(nc.psum_tensor(name, [P, 512], F32))

        def sem(name):
            return ctx.enter_context(nc.semaphore(name))

        ident = sb("ident", [P, P])
        upto = sb("upto", [P, P])
        after = sb("after", [P, P])
        ones = sb("ones", [P, P])
        iota8 = sb("iota8", [P, E])
        tick = sb("tick", [P, 1])
        copy_rows = sb("copy_rows", [P, 4])
        ln_eps = sb("ln_eps", [P, 1])
        scan_eps = sb("scan_eps", [P, 1])
        wqk_s = sb("wqk_s", [P, HG, 2, P])
        wv_s = sb("wv_s", [P, P])
        bqk_s = sb("bqk_s", [P, HG, 2])
        bqk_m = sb("bqk_m", [P, HG, 2])
        bv_s = sb("bv_s", [P, P])
        wo_s = sb("wo_s", [P, P])
        bo_s = sb("bo_s", [P, P])
        wx_s = sb("wx_s", [P, R + 2 * N])
        wdt_s = sb("wdt_s", [R, P])
        bdt_s = sb("bdt_s", [P, P])
        Abc = sb("Abc", [P, N * D])
        D_s = sb("D_s", [P, P])
        wout_s = sb("wout_s", [P, P])
        bout_s = sb("bout_s", [P, P])
        gate_s = sb("gate_s", [P, E])
        w1_h = sb("w1_h", [P, E * FF], F32R)
        w1_l = sb("w1_l", [P, E * FF], F32R)
        w2_h = sb("w2_h", [P, E * FC * P], F32R)
        w2_l = sb("w2_l", [P, E * FC * P], F32R)

        xin = sb("xin", [P, T, P])
        x1 = sb("x1", [P, T, P])
        x2 = sb("x2", [P, T, P])
        x3 = sb("x3", [P, T, P])
        xo = sb("xo", [P, T, P])
        a_st = sb("a_st", [P, T, 6])
        a_mv = sb("a_mv", [P, T, 2])
        a_lv = sb("a_lv", [P, T])
        a_rs = sb("a_rs", [P, T])
        a_xn = sb("a_xn", [P, T, P])
        a_xnT = sb("a_xnT", [P, L])
        qk = sb("qk", [P, HG, 2, L], F32R)
        v_s = sb("v_s", [P, T, P])
        nmx = sb("nmx", [P, T, H])
        Z = sb("Z", [P, T, H])
        rz = sb("rz", [P, T, H])
        attsum = sb("attsum", [P, T, H])
        probs = sb("probs", [P, NSC, T, L], BF16)
        xb1 = sb("xb1", [P, T, P])
        s_st = sb("s_st", [P, T, 6])
        s_mv = sb("s_mv", [P, T, 2])
        s_lv = sb("s_lv", [P, T])
        s_rs = sb("s_rs", [P, T])
        u_s = sb("u_s", [P, T, P])
        uT = sb("uT", [P, L])
        dlrT = sb("dlrT", [R, L])
        bc = sb("bc", [P, T, 2 * N])
        dpre = sb("dpre", [P, T, P])
        dneg = sb("dneg", [P, T, P])
        delta = sb("delta", [P, T, P])
        du = sb("du", [P, T, P])
        Rs = sb("Rs", [P, T, P])
        Ea = sb("Ea", [P, T, N * D])
        rr = sb("rr", [P, T, N * D])
        Pb = sb("Pb", [P, T, N * D])
        y_s = sb("y_s", [P, T, P])
        uD = sb("uD", [P, T, P])
        xb2 = sb("xb2", [P, T, P])
        p_st = sb("p_st", [P, T, 6])
        p_mv = sb("p_mv", [P, T, 2])
        p_lv = sb("p_lv", [P, T])
        p_rs = sb("p_rs", [P, T])
        p_xn = sb("p_xn", [P, T, P])
        p_xnT = sb("p_xnT", [P, L])
        lg = sb("lg", [P, T, E])
        top = sb("top", [P, T, 8])
        topi = sb("topi", [P, T, 8], U32)
        tdiff = sb("tdiff", [P, T, 2])
        texp = sb("texp", [P, T, 2])
        tsum = sb("tsum", [P, T])
        trec = sb("trec", [P, T])
        tw = sb("tw", [P, T, 2])
        hot = sb("hot", [P, T, 2, E])
        hotw = sb("hotw", [P, T, 2, E])
        comb = sb("comb", [P, T, E])
        xs = sb("xs", [P, T, E, P])
        xsT_h = sb("xsT_h", [P, E, L], F32R)
        xsT_l = sb("xsT_l", [P, E, L], F32R)
        hid_h = sb("hid_h", [P, 2, FC, L], F32R)
        hid_l = sb("hid_l", [P, 2, FC, L], F32R)
        accT = sb("accT", [P, L])

        w1_s = rr[:].rearrange("p c n -> p (c n)")
        w2_s = Pb[:].rearrange("p c n -> p (c n)")

        hb = [bank("h_bank0"), bank("h_bank1")]
        acc = bank("acc_bank")
        sc = [bank(f"sc_bank{n}") for n in range(NSC)]
        ma = bank("mix_bank")
        mp = bank("prep_bank")

        w_attn, w_scan, w_gate, w_w1, w_w2 = (sem(f"w_{n}") for n in ("attn", "scan", "gate", "w1", "w2"))
        c_pool, c_dve, c_act = sem("const_pool"), sem("const_dve"), sem("const_act")
        s_xin = sem("xin_loaded")
        s_out = sem("out_stored")

        rounds = range(ROUNDS)
        GROUP_HALVES = range(1, 1 + HG)
        V_HALF = 5
        ROUND_HALVES = range(3, 15)

        def attn_rounds(half):
            if half not in ROUND_HALVES:
                return range(0)
            n, k = len(ROUND_HALVES), half - ROUND_HALVES[0]
            return range(k * ROUNDS // n, (k + 1) * ROUNDS // n)

        def in_halves(group, v, score, later=0):
            events = []
            for half in range(HALVES + 1):
                if half in GROUP_HALVES:
                    events.append(f"{group}{half - 1}")
                if half == V_HALF and v:
                    events.append(v)
                events += [f"{score}{r}" for r in attn_rounds(half - later)]
            return events

        attn_dve = Progress(sem("attn_dve"), ["st0", "stats0", "stats1", "xn0", "xn"] + in_halves("qk", "v", "max")
                            + ["rz", "attsum", "o", "x1"])
        attn_act = Progress(sem("attn_act"), ["ln", "rstd", "xnT"] + in_halves("qk", None, "exp", 1) + ["oT"])
        attn_pe = Progress(sem("attn_pe"), ["xnT"] + in_halves("qk", "v", "score") + ["oT", "out"])
        attn_pool = Progress(sem("attn_pool"), ["xb"])

        chunks = range(CHUNKS)
        scan_dve = Progress(sem("scan_dve"), ["st0", "stats0", "stats1", "u0", "u", "dpre", "dneg", "delta", "du", "P0", "P1", "P2", "X0", "P3",
                                              "X1", "P4", "X2", "P5", "X3", "P6", "X4", "y0", "P7", "X5", "X6", "X7", "y", "yD", "x3"])
        scan_act = Progress(sem("scan_act"), ["ln", "rstd", "uT", "dlr", "bc", "exp", "log", "R", "E0"]
                            + [f"{w}{k - (w != 'E')}" for k in range(1, CHUNKS) for w in "ELr"] + [f"L{CHUNKS - 1}", f"r{CHUNKS - 1}", "yT"])
        scan_pe = Progress(sem("scan_pe"), ["uT", "xdbl", "dpre", "R"] + [f"S{k}" for k in chunks] + ["yT", "out"])
        scan_pool = Progress(sem("scan_pool"), [f"arg{k}" for k in chunks] + ["uD", "xb"])

        prep_dve, prep_act, prep_pe, prep_pool, exp_pe, exp_act, exp_dve, fin_pe, fin_act, fin_dve = ({} for _ in range(10))
        for ly in (1, 2):
            prep_dve[ly] = Progress(sem(f"prep{ly}_dve"), ["st0", "stats0", "stats1", "xn0", "xn", "lg", "top0", "top1", "topi",
                                                           "diff", "sum", "rec", "w", "hot", "hotw", "comb"]
                                    + [f"xs{r}" for r in range(E // 2)])
            prep_act[ly] = Progress(sem(f"prep{ly}_act"), ["ln", "rstd", "xnT", "texp"] + [f"xs{r}" for r in range(E // 2)])
            prep_pe[ly] = Progress(sem(f"prep{ly}_pe"), ["xnT", "lg"] + [f"xs{r}" for r in range(E // 2)])
            prep_pool[ly] = Progress(sem(f"prep{ly}_pool"), ["xs0", "xs1"])
            exp_pe[ly] = Progress(sem(f"exp{ly}_pe"), [f"h{e}{w}" for e in range(E) for w in range(2)] + ["sum"])
            exp_act[ly] = Progress(sem(f"exp{ly}_act"), [f"h{e}{w}" for e in range(E) for w in range(2)])
            exp_dve[ly] = Progress(sem(f"exp{ly}_dve"), [f"h{e}{w}" for e in range(E) for w in range(2)])
            fin_pe[ly] = Progress(sem(f"fin{ly}_pe"), ["t"])
            fin_act[ly] = Progress(sem(f"fin{ly}_act"), ["acc"])
            fin_dve[ly] = Progress(sem(f"fin{ly}_dve"), ["x"])

        def has(b):
            return not isinstance(b, int) or 0 <= b < NSEQ

        def wait_latest(eng, *uses):
            for progress, event, b in uses:
                if has(b):
                    eng.wait_ge(*progress.at(event, b))
                    return

        def previous_pass(ly, b):
            return ((2, b - 2), (1, b - 1)) if ly == 1 else ((1, b + 1), (2, b - 1))

        PREP_ROUNDS = {13: 0, 14: 1, 15: 2, 16: 3}

        def run(eng, phase1, phase2):
            def step(i):
                phase1(i)
                phase2(i)
            for i in range(4):
                step(i)
            with eng.Fori(4, NSEQ - 1) as i:
                step(i)
            for i in range(NSEQ - 1, NSEQ + 3):
                step(i)

        last_round = [max(r for r in rounds if r % NSC == n) for n in range(NSC)]
        last_chunk = [max(k for k in chunks if k % NSC == n) for n in range(NSC)]

        def round_bank(r):
            return (mp, ma)[r % 2]

        def qk_bank(g):
            return (ma, mp)[g % 2]

        def quarter(k):
            return k // 4, slice((k % 4) * 512, (k % 4 + 1) * 512), range((k % 4) * 4, (k % 4) * 4 + 4)

        block = ctx.enter_context(nc.Block())

        @block.sync
        def _(sp):
            def load_x(b):
                if not isinstance(b, int) or b > 0:
                    sp.wait_ge(*attn_pool.at("xb", b - 1))
                sp.dma_start(xin[:], x_v[b]).then_inc(s_xin, 16)

            def store(b):
                sp.wait_ge(*fin_dve[2].at("x", b))
                sp.dma_start(out_v[b], xo[:]).then_inc(s_out, 16)

            load_x(0)
            for dst, src in ((wqk_s, wqkT), (wv_s, wvT), (bqk_s, b_qk), (wo_s, woT)):
                sp.dma_start(dst[:], src).then_inc(w_attn, 16)
            for dst, src in ((bv_s, b_v), (bo_s, b_o)):
                sp.dma_start(dst[:], src.partition_broadcast(P)).then_inc(w_attn, 16)
            sp.dma_start(gate_s[:], gate_w).then_inc(w_gate, 16)
            sp.dma_start(w1_s.rearrange("p (e f) -> p e f", e=E), w1.rearrange("e d f -> d e f")).then_inc(w_w1, 16)
            sp.dma_start(w2_s.rearrange("p (e k d) -> p e k d", e=E, k=FC),
                         w2.rearrange("e (k f) d -> f e k d", f=P)).then_inc(w_w2, 16)

            def phase1(i):
                if has(i - 3):
                    store(i - 3)

            def phase2(i):
                if not isinstance(i, int) or i + 1 < NSEQ:
                    load_x(i + 1)

            for i in range(4):
                phase1(i)
                phase2(i)
            with sp.Fori(4, NSEQ - 1) as i:
                phase1(i)
                phase2(i)
            for i in range(NSEQ - 1, NSEQ + 3):
                phase1(i)
                phase2(i)
            sp.wait_ge(s_out, 16 * NSEQ)

        W_ATTN = 16 * 6
        W_SCAN = 16 * 7

        @block.gpsimd
        def _(pool):
            for dst, src in ((wx_s, W_x), (wdt_s, W_dt), (wout_s, W_out)):
                pool.dma_start(dst[:], src).then_inc(w_scan, 16)
            for dst, src in ((bdt_s, b_dt), (Abc, A_logT), (D_s, D_skip), (bout_s, b_out2)):
                pool.dma_start(dst[:], src.partition_broadcast(P)).then_inc(w_scan, 16)
            pool.memset(ident[:], 0.0).then_inc(c_pool, 1)
            pool.memset(upto[:], 1.0).then_inc(c_pool, 1)
            pool.memset(after[:], 1.0).then_inc(c_pool, 1)
            pool.memset(ones[:], 1.0).then_inc(c_pool, 1)
            for e in range(E):
                pool.memset(iota8[:, e:e + 1], float(e)).then_inc(c_pool, 1)
            pool.memset(ln_eps[:], LN_EPS).then_inc(c_pool, 1)
            pool.memset(scan_eps[:], SCAN_EPS).then_inc(c_pool, 1)
            pool.wait_ge(c_pool, 6 + E)
            pool.affine_select(out=ident[:], in_=ident[:], compare_op=ALU.not_equal, fill=1.0, base=0,
                               pattern=[[-1, P]], channel_multiplier=1).then_inc(c_pool, 1)
            pool.affine_select(out=upto[:], in_=upto[:], compare_op=ALU.is_ge, fill=0.0, base=0,
                               pattern=[[1, P]], channel_multiplier=-1).then_inc(c_pool, 1)
            pool.affine_select(out=after[:], in_=after[:], compare_op=ALU.is_gt, fill=0.0, base=0,
                               pattern=[[-1, P]], channel_multiplier=1).then_inc(c_pool, 1)
            pool.wait_ge(w_attn, W_ATTN)
            pool.wait_ge(w_scan, W_SCAN)

            def attn_residual(b):
                pool.wait_ge(s_xin, 16 * (b + 1))
                wait_latest(pool, (attn_dve, "x1", b - 1))
                pool.wait_ge(*attn_dve.at("xn", b))
                pool.tensor_tensor(xb1[:], xin[:], bo_s[:].unsqueeze(1).broadcast_to([P, T, P]),
                                   ALU.add).then_inc(*attn_pool.done("xb"))

            def scan_exponents(b, k):
                c, s, _ = quarter(k)
                if k == 0:
                    pool.wait_ge(*scan_act.at("R", b))
                    pool.wait_ge(c_dve, 6)
                    wait_latest(pool, (scan_dve, "y", b - 1))
                pool.tensor_tensor(Ea[:, c, s].rearrange("p (n d) -> p n d", d=D), Rs[:, c].unsqueeze(1).broadcast_to([P, 4, D]),
                                   Abc[:, s].rearrange("p (n d) -> p n d", d=D), ALU.mult).then_inc(*scan_pool.done(f"arg{k}"))

            def scan_rest(b):
                pool.wait_ge(*scan_dve.at("u", b))
                wait_latest(pool, (scan_dve, "x3", b - 1))
                pool.tensor_tensor(uD[:], u_s[:], D_s[:].unsqueeze(1).broadcast_to([P, T, P]),
                                   ALU.mult).then_inc(*scan_pool.done("uD"))
                pool.tensor_tensor(xb2[:], x2[:], bout_s[:].unsqueeze(1).broadcast_to([P, T, P]),
                                   ALU.add).then_inc(*scan_pool.done("xb"))

            def prep_scale(ly, b, c):
                pool.wait_ge(*prep_dve[ly].at("comb", b))
                if c == 0:
                    if ly == 2:
                        wait_latest(pool, (prep_pe[1], f"xs{E // 2 - 1}", b + 1), (prep_pe[2], f"xs{E // 2 - 1}", b - 1))
                    else:
                        wait_latest(pool, (prep_pe[2], f"xs{E // 2 - 1}", b - 2), (prep_pe[1], f"xs{E // 2 - 1}", b - 1))
                pool.tensor_tensor(xs[:, c], p_xn[:, c].unsqueeze(1).broadcast_to([P, E, P]),
                                   comb[:, c].unsqueeze(2).broadcast_to([P, E, P]),
                                   ALU.mult).then_inc(*prep_pool[ly].done(f"xs{c}"))

            def phase1(i):
                if has(i):
                    attn_residual(i)
                if has(i - 2):
                    prep_scale(2, i - 2, 0)
                    prep_scale(2, i - 2, 1)

            def phase2(i):
                if has(i - 1):
                    for k in range(3):
                        scan_exponents(i - 1, k)
                if has(i):
                    prep_scale(1, i, 0)
                if has(i - 1):
                    scan_exponents(i - 1, 3)
                if has(i):
                    prep_scale(1, i, 1)
                if has(i - 1):
                    for k in range(4, CHUNKS):
                        scan_exponents(i - 1, k)
                    scan_rest(i - 1)

            run(pool, phase1, phase2)

        @block.scalar
        def _(act):
            act.preload_act_table_set("natural_log_exp_and_others")
            act.wait_ge(c_pool, 6 + E + 3)
            act.wait_ge(w_scan, W_SCAN)
            act.activation(Abc[:], Abc[:], ACT.Exp).then_inc(c_act, 1)
            act.wait_ge(w_w1, 16)
            act.activation(w1_h[:], w1_s, ACT.Copy).then_inc(c_act, 1)
            act.wait_ge(w_w2, 16)
            act.activation(w2_h[:], w2_s, ACT.Copy).then_inc(c_act, 1)

            def rstd(progress, dve, b, mv, lv, rs):
                act.wait_ge(*dve.at("stats1", b))
                act.activation(lv[:], mv[:, :, 1], ACT.Ln, bias=ln_eps[:]).then_inc(*progress.done("ln"))
                act.wait_ge(*progress.at("ln", b))
                act.activation(rs[:], lv[:], ACT.Exp, scale=-0.5).then_inc(*progress.done("rstd"))

            def attn_xnT(b):
                act.wait_ge(*attn_pe.at("xnT", b))
                act.activation(a_xnT[:], ma[:, 0:L], ACT.Copy).then_inc(*attn_act.done("xnT"))

            def attn_qk(b, g):
                act.wait_ge(*attn_pe.at(f"qk{g}", b))
                if g == 0:
                    act.wait_ge(c_dve, 5)
                for n in range(2):
                    last = act.activation(qk[:, g, n, :], qk_bank(g)[:, n * L:(n + 1) * L], ACT.Identity, bias=bqk_m[:, g, n:n + 1],
                                          scale=copy_rows[:, LOW_COPY[n]:LOW_COPY[n] + 1])
                last.then_inc(*attn_act.done(f"qk{g}"))

            def attn_exp(b, r):
                act.wait_ge(*attn_dve.at(f"max{r}", b))
                for c in range(T):
                    last = act.activation(probs[:, r % NSC, c], sc[r % NSC][:, c * L:(c + 1) * L], ACT.Exp, bias=nmx[:, c, r:r + 1],
                                          accum_out=Z[:, c, r:r + 1])
                last.then_inc(*attn_act.done(f"exp{r}"))

            def attn_oT(b):
                act.wait_ge(*attn_pe.at("oT", b))
                act.activation(a_xnT[:], ma[:, 0:L], ACT.Copy).then_inc(*attn_act.done("oT"))

            def scan_uT(b):
                act.wait_ge(*scan_pe.at("uT", b))
                act.activation(uT[:], ma[:, 0:L], ACT.Copy).then_inc(*scan_act.done("uT"))

            def scan_xdbl(b):
                act.wait_ge(*scan_pe.at("xdbl", b))
                act.activation(dlrT[:], ma[0:R, 0:L], ACT.Copy).then_inc(*scan_act.done("dlr"))
                act.activation(bc[:], ma[:, L:L + T * 2 * N].rearrange("p (c n) -> p c n", c=T),
                               ACT.Copy).then_inc(*scan_act.done("bc"))

            def scan_softplus(b):
                act.wait_ge(*scan_dve.at("dneg", b))
                act.activation(dneg[:], dneg[:], ACT.Exp).then_inc(*scan_act.done("exp"))
                act.wait_ge(*scan_act.at("exp", b))
                act.activation(dneg[:], dneg[:], ACT.Ln, bias=ones[:, 0:1]).then_inc(*scan_act.done("log"))

            def scan_R(b):
                act.wait_ge(*scan_pe.at("R", b))
                act.activation(Rs[:], ma[:, 0:T * P].rearrange("p (c d) -> p c d", c=T),
                               ACT.Copy).then_inc(*scan_act.done("R"))

            def scan_E(b, k):
                c, s, _ = quarter(k)
                act.wait_ge(*scan_pool.at(f"arg{k}", b))
                act.activation(Ea[:, c, s], Ea[:, c, s], ACT.Exp).then_inc(*scan_act.done(f"E{k}"))

            def scan_L(b, k):
                c, s, _ = quarter(k)
                act.wait_ge(*scan_act.at(f"E{k}", b))
                if k == 0:
                    wait_latest(act, (scan_dve, f"X{CHUNKS - 1}", b - 1))
                act.activation(rr[:, c, s], Ea[:, c, s], ACT.Ln, bias=scan_eps[:]).then_inc(*scan_act.done(f"L{k}"))

            def scan_r(b, k):
                c, s, _ = quarter(k)
                act.wait_ge(*scan_act.at(f"L{k}", b))
                act.activation(rr[:, c, s], rr[:, c, s], ACT.Exp, scale=-1.0).then_inc(*scan_act.done(f"r{k}"))

            def scan_exps(b, k):
                if k < CHUNKS:
                    scan_E(b, k)
                if k > 0:
                    scan_L(b, k - 1)
                    scan_r(b, k - 1)

            def scan_yT(b):
                act.wait_ge(*scan_pe.at("yT", b))
                act.activation(uT[:], mp[:, 0:L], ACT.Copy).then_inc(*scan_act.done("yT"))

            def prep_xnT(ly, b):
                act.wait_ge(*prep_pe[ly].at("xnT", b))
                act.activation(p_xnT[:], mp[:, 0:L], ACT.Copy).then_inc(*prep_act[ly].done("xnT"))

            def prep_texp(ly, b):
                act.wait_ge(*prep_dve[ly].at("diff", b))
                act.activation(texp[:], tdiff[:], ACT.Exp).then_inc(*prep_act[ly].done("texp"))

            def prep_xsT(ly, b, r):
                act.wait_ge(*prep_pe[ly].at(f"xs{r}", b))
                wait_latest(act, *((exp_pe[l], f"h{2 * r + 1}1", n) for l, n in previous_pass(ly, b)))
                act.activation(xsT_h[:, 2 * r:2 * r + 2, :], round_bank(r)[:].rearrange("p (e t) -> p e t", e=2),
                               ACT.Copy).then_inc(*prep_act[ly].done(f"xs{r}"))

            def fin_acc(ly, b):
                act.wait_ge(*exp_pe[ly].at("sum", b))
                act.activation(accT[:], acc[:, 0:L], ACT.Copy).then_inc(*fin_act[ly].done("acc"))

            def hidden(ly, b, e, w):
                act.wait_ge(*exp_pe[ly].at(f"h{e}{w}", b))
                act.activation(hid_h[:, e % 2, 2 * w:2 * w + 2, :], hb[w][:].rearrange("p (k t) -> p k t", k=2),
                               ACT.Relu).then_inc(*exp_act[ly].done(f"h{e}{w}"))

            def phase1(i):
                for half in range(HALVES + 1):
                    if half % 2 == 1 and has(i - 1):
                        hidden(1, i - 1, half // 2, 1)
                    if half == 0 and has(i - 3):
                        fin_acc(2, i - 3)
                    if half <= 1 and has(i - 2):
                        scan_exps(i - 2, 7 + half)
                    if half == 0 and has(i):
                        if isinstance(i, int) and i == 0:
                            rstd(attn_act, attn_dve, 0, a_mv, a_lv, a_rs)
                        attn_xnT(i)
                    if half in GROUP_HALVES and has(i):
                        attn_qk(i, half - 1)
                    if half == 5 and has(i - 2):
                        scan_yT(i - 2)
                    if half == 7 and has(i - 2):
                        rstd(prep_act[2], prep_dve[2], i - 2, p_mv, p_lv, p_rs)
                    if half == 8 and has(i - 2):
                        prep_xnT(2, i - 2)
                    if half == 10 and has(i - 2):
                        prep_texp(2, i - 2)
                    if half in PREP_ROUNDS and has(i - 2):
                        prep_xsT(2, i - 2, PREP_ROUNDS[half])
                    if has(i):
                        for r in attn_rounds(half - 1):
                            attn_exp(i, r)
                    if half % 2 == 0 and half < HALVES and has(i - 1):
                        hidden(1, i - 1, half // 2, 0)

            def phase2(i):
                for half in range(HALVES + 1):
                    if half % 2 == 1 and has(i - 2):
                        hidden(2, i - 2, half // 2, 1)
                    if half == 0 and has(i - 1):
                        fin_acc(1, i - 1)
                    if half == 0 and has(i):
                        attn_oT(i)
                    if half == 2 and has(i - 1):
                        rstd(scan_act, scan_dve, i - 1, s_mv, s_lv, s_rs)
                    if half == 3 and has(i - 1):
                        scan_uT(i - 1)
                    if half == 4 and has(i - 1):
                        scan_xdbl(i - 1)
                    if half == 3 and has(i):
                        rstd(prep_act[1], prep_dve[1], i, p_mv, p_lv, p_rs)
                    if half == 4 and has(i):
                        prep_xnT(1, i)
                    if half == 6 and has(i - 1):
                        scan_softplus(i - 1)
                    if half == 6 and has(i):
                        prep_texp(1, i)
                    if half == 8 and has(i - 1):
                        scan_R(i - 1)
                    if half in PREP_ROUNDS and has(i):
                        prep_xsT(1, i, PREP_ROUNDS[half])
                    if 9 <= half < HALVES and has(i - 1):
                        scan_exps(i - 1, half - 9)
                    if half == 15 and has(i + 1):
                        rstd(attn_act, attn_dve, i + 1, a_mv, a_lv, a_rs)
                    if half % 2 == 0 and half < HALVES and has(i - 2):
                        hidden(2, i - 2, half // 2, 0)

            run(act, phase1, phase2)

        @block.vector
        def _(dve):
            dve.wait_ge(c_pool, 6 + E + 3)
            dve.tensor_reduce(copy_rows[:], ident[:].rearrange("p (j r d) -> p r j d", j=HG, d=DH), AX.XY,
                              ALU.add).then_inc(c_dve, 1)
            dve.wait_ge(w_attn, W_ATTN)
            dve.tensor_scalar(wqk_s[:, :, 0, :], wqk_s[:, :, 0, :], SCALE, None, ALU.mult).then_inc(c_dve, 1)
            dve.tensor_scalar(bqk_s[:, :, 0], bqk_s[:, :, 0], SCALE, None, ALU.mult).then_inc(c_dve, 1)
            dve.wait_ge(c_dve, 3)
            for n in range(2):
                r = LOW_COPY[n]
                dve.tensor_scalar(bqk_m[:, :, n], bqk_s[:, :, n], copy_rows[:, r:r + 1], None, ALU.mult).then_inc(c_dve, 1)
            dve.wait_ge(c_act, 1)
            dve.tensor_scalar(Abc[:], Abc[:], -1.0, None, ALU.mult).then_inc(c_dve, 1)
            dve.wait_ge(c_dve, 6)
            dve.wait_ge(w_scan, W_SCAN)
            dve.wait_ge(c_act, 2)
            dve.tensor_tensor(w1_l[:], w1_s, w1_h[:].bitcast(F32), ALU.subtract).then_inc(c_dve, 1)
            dve.wait_ge(c_act, 3)
            dve.tensor_tensor(w2_l[:], w2_s, w2_h[:].bitcast(F32), ALU.subtract).then_inc(c_dve, 1)

            def stats(progress, b, src, st, mv):
                dve.bn_stats(st[:, 0, :], src[:, 0, :])
                dve.bn_stats(st[:, 1, :], src[:, 1, :]).then_inc(*progress.done("st0"))
                dve.wait_ge(*progress.at("st0", b))
                dve.memset(tick[:], 0.0)
                dve.bn_aggr(mv[:, 0, :], st[:, 0, :]).then_inc(*progress.done("stats0"))
                dve.bn_aggr(mv[:, 1, :], st[:, 1, :]).then_inc(*progress.done("stats1"))

            def normalise(progress, act_progress, b, src, mv, rs, dst, events):
                dve.wait_ge(*act_progress.at("rstd", b))
                for c in range(T):
                    dve.tensor_scalar(dst[:, c, :], src[:, c, :], mv[:, c, 0:1], rs[:, c:c + 1], ALU.subtract,
                                      ALU.mult).then_inc(*progress.done(events[c]))

            def attn_stats(b):
                dve.wait_ge(s_xin, 16 * (b + 1))
                stats(attn_dve, b, xin, a_st, a_mv)

            def attn_norm(b):
                normalise(attn_dve, attn_act, b, xin, a_mv, a_rs, a_xn, ("xn0", "xn"))

            def attn_qk(b, g):
                dve.wait_ge(*attn_act.at(f"qk{g}", b))
                for n in range(2):
                    last = dve.scalar_tensor_tensor(out=qk[:, g, n, :], in0=qk_bank(g)[:, n * L:(n + 1) * L],
                                                    scalar=bqk_s[:, g, n:n + 1], in1=qk[:, g, n, :].bitcast(F32), op0=ALU.add,
                                                    op1=ALU.subtract)
                last.then_inc(*attn_dve.done(f"qk{g}"))

            def attn_v(b):
                dve.wait_ge(*attn_pe.at("v", b))
                dve.tensor_tensor(v_s[:], ma[:, 0:T * P].rearrange("p (c d) -> p c d", c=T),
                                  bv_s[:].unsqueeze(1).broadcast_to([P, T, P]), ALU.add).then_inc(*attn_dve.done("v"))

            def attn_max(b, r):
                dve.wait_ge(*attn_pe.at(f"score{r}", b))
                dve.tensor_reduce(nmx[:, :, r], sc[r % NSC][:].rearrange("p (c m) -> p c m", c=T), AX.X, ALU.max,
                                  negate=True).then_inc(*attn_dve.done(f"max{r}"))

            def attn_out(b):
                dve.wait_ge(*attn_act.at(f"exp{ROUNDS - 1}", b))
                dve.reciprocal(rz[:], Z[:]).then_inc(*attn_dve.done("rz"))
                dve.wait_ge(*attn_dve.at("rz", b))
                dve.tensor_tensor(attsum[:], Z[:], rz[:], ALU.mult).then_inc(*attn_dve.done("attsum"))
                dve.wait_ge(*attn_dve.at("attsum", b))
                dve.tensor_tensor(v_s[:].rearrange("p c (h d) -> p (c h) d", d=DH), v_s[:].rearrange("p c (h d) -> p (c h) d", d=DH),
                                  attsum[:].rearrange("p c h -> p (c h)").unsqueeze(2).broadcast_to([P, T * H, DH]),
                                  ALU.mult).then_inc(*attn_dve.done("o"))

            def attn_add(b):
                dve.wait_ge(*attn_pe.at("out", b))
                wait_latest(dve, (fin_dve[1], "x", b - 1))
                dve.wait_ge(*attn_pool.at("xb", b))
                dve.tensor_tensor(x1[:], mp[:, 0:T * P].rearrange("p (c d) -> p c d", c=T), xb1[:],
                                  ALU.add).then_inc(*attn_dve.done("x1"))

            def scan_stats(b):
                dve.wait_ge(*fin_dve[1].at("x", b))
                stats(scan_dve, b, x2, s_st, s_mv)

            def scan_norm(b):
                normalise(scan_dve, scan_act, b, x2, s_mv, s_rs, u_s, ("u0", "u"))

            def scan_dpre(b):
                dve.wait_ge(*scan_pe.at("dpre", b))
                dve.tensor_tensor(dpre[:], ma[:, 0:T * P].rearrange("p (c d) -> p c d", c=T),
                                  bdt_s[:].unsqueeze(1).broadcast_to([P, T, P]), ALU.add).then_inc(*scan_dve.done("dpre"))
                dve.wait_ge(*scan_dve.at("dpre", b))
                dve.scalar_tensor_tensor(out=dneg[:], in0=dpre[:], scalar=-1.0, in1=dpre[:], op0=ALU.mult,
                                         op1=ALU.min).then_inc(*scan_dve.done("dneg"))

            def scan_delta(b):
                dve.wait_ge(*scan_act.at("log", b))
                dve.scalar_tensor_tensor(out=delta[:], in0=dpre[:], scalar=0.0, in1=dneg[:], op0=ALU.max,
                                         op1=ALU.add).then_inc(*scan_dve.done("delta"))
                dve.wait_ge(*scan_dve.at("delta", b))
                dve.tensor_tensor(du[:], delta[:], u_s[:], ALU.mult).then_inc(*scan_dve.done("du"))

            def scan_inputs(b, k):
                c, _, states = quarter(k)
                dve.wait_ge(*scan_act.at(f"E{k}", b))
                if k == 0:
                    dve.wait_ge(*scan_dve.at("du", b))
                for n in states:
                    s = slice(n * D, (n + 1) * D)
                    last = dve.scalar_tensor_tensor(out=Pb[:, c, s], in0=Ea[:, c, s], scalar=bc[:, c, n:n + 1],
                                                    in1=du[:, c, :], op0=ALU.mult, op1=ALU.mult)
                last.then_inc(*scan_dve.done(f"P{k}"))

            def scan_weigh(b, k):
                c, _, states = quarter(k)
                dve.wait_ge(*scan_pe.at(f"S{k}", b))
                dve.wait_ge(*scan_act.at(f"r{k}", b))
                for n in states:
                    s = slice(n * D, (n + 1) * D)
                    last = dve.scalar_tensor_tensor(out=Ea[:, c, s], in0=sc[k % NSC][:, (n % 4) * D:(n % 4 + 1) * D],
                                                    scalar=bc[:, c, N + n:N + n + 1], in1=rr[:, c, s], op0=ALU.mult, op1=ALU.mult)
                last.then_inc(*scan_dve.done(f"X{k}"))

            def scan_y(b, c):
                dve.wait_ge(*scan_dve.at(f"X{4 * c + 3}", b))
                dve.tensor_reduce(y_s[:, c, :], Ea[:, c].rearrange("p (n d) -> p d n", n=N), AX.X,
                                  ALU.add).then_inc(*scan_dve.done("y" if c else "y0"))

            def scan_skip(b):
                dve.wait_ge(*scan_pool.at("uD", b))
                dve.wait_ge(*scan_dve.at("y", b))
                dve.tensor_tensor(y_s[:], y_s[:], uD[:], ALU.add).then_inc(*scan_dve.done("yD"))

            def scan_add(b):
                dve.wait_ge(*scan_pe.at("out", b))
                wait_latest(dve, (fin_dve[2], "x", b - 1))
                dve.wait_ge(*scan_pool.at("xb", b))
                dve.tensor_tensor(x3[:], mp[:, 0:T * P].rearrange("p (c d) -> p c d", c=T), xb2[:],
                                  ALU.add).then_inc(*scan_dve.done("x3"))

            def prep_stats(ly, b):
                src = x1 if ly == 1 else x3
                dve.wait_ge(*(attn_dve.at("x1", b) if ly == 1 else scan_dve.at("x3", b)))
                stats(prep_dve[ly], b, src, p_st, p_mv)

            def prep_norm(ly, b):
                src = x1 if ly == 1 else x3
                if ly == 2:
                    wait_latest(dve, (prep_pool[1], "xs1", b + 1), (prep_pool[2], "xs1", b - 1))
                else:
                    wait_latest(dve, (prep_pool[2], "xs1", b - 2), (prep_pool[1], "xs1", b - 1))
                normalise(prep_dve[ly], prep_act[ly], b, src, p_mv, p_rs, p_xn, ("xn0", "xn"))

            def prep_top(ly, b):
                pr = prep_dve[ly]
                dve.wait_ge(*prep_pe[ly].at("lg", b))
                dve.tensor_copy(lg[:], mp[:, L:L + T * E].rearrange("p (c e) -> p c e", c=T)).then_inc(*pr.done("lg"))
                dve.wait_ge(*pr.at("lg", b))
                dve.memset(tick[:], 0.0)
                dve.max(top[:, 0, :], lg[:, 0, :]).then_inc(*pr.done("top0"))
                dve.max(top[:, 1, :], lg[:, 1, :]).then_inc(*pr.done("top1"))
                dve.wait_ge(*pr.at("top1", b))
                dve.memset(tick[:], 0.0)
                dve.max_index(topi[:, 0, :], top[:, 0, :], lg[:, 0, :])
                dve.max_index(topi[:, 1, :], top[:, 1, :], lg[:, 1, :]).then_inc(*pr.done("topi"))
                dve.tensor_tensor(tdiff[:], top[:, :, 0:2], top[:, :, 0:1].broadcast_to([P, T, 2]),
                                  ALU.subtract).then_inc(*pr.done("diff"))

            def prep_weights(ly, b):
                pr = prep_dve[ly]
                dve.wait_ge(*prep_act[ly].at("texp", b))
                dve.tensor_reduce(tsum[:], texp[:], AX.X, ALU.add).then_inc(*pr.done("sum"))
                dve.wait_ge(*pr.at("sum", b))
                dve.reciprocal(trec[:], tsum[:]).then_inc(*pr.done("rec"))
                dve.wait_ge(*pr.at("rec", b))
                dve.tensor_tensor(tw[:], texp[:], trec[:].unsqueeze(2).broadcast_to([P, T, 2]), ALU.mult).then_inc(*pr.done("w"))
                for c in range(T):
                    last = dve.tensor_tensor(hot[:, c], topi[:, c, 0:2].unsqueeze(2).broadcast_to([P, 2, E]),
                                             iota8[:].unsqueeze(1).broadcast_to([P, 2, E]), ALU.is_equal)
                last.then_inc(*pr.done("hot"))
                dve.wait_ge(*pr.at("hot", b))
                dve.tensor_tensor(hotw[:].rearrange("p c k e -> p (c k) e"), hot[:].rearrange("p c k e -> p (c k) e"),
                                  tw[:].rearrange("p c k -> p (c k)").unsqueeze(2).broadcast_to([P, 2 * T, E]),
                                  ALU.mult).then_inc(*pr.done("hotw"))
                dve.wait_ge(*pr.at("hotw", b))
                dve.tensor_tensor(comb[:], hotw[:, :, 0, :], hotw[:, :, 1, :], ALU.add).then_inc(*pr.done("comb"))

            def fin_add(ly, b):
                dve.wait_ge(*fin_pe[ly].at("t", b))
                src, dst = (x1, x2) if ly == 1 else (x3, xo)
                if ly == 1:
                    wait_latest(dve, (scan_pool, "xb", b - 1))
                elif not isinstance(b, int) or b > 0:
                    dve.wait_ge(s_out, 16 * b)
                dve.tensor_tensor(dst[:], mp[:, 0:T * P].rearrange("p (c d) -> p c d", c=T), src[:],
                                  ALU.add).then_inc(*fin_dve[ly].done("x"))

            def prep_low(ly, b, r):
                dve.wait_ge(*prep_act[ly].at(f"xs{r}", b))
                e = slice(2 * r, 2 * r + 2)
                dve.tensor_tensor(xsT_l[:, e, :], round_bank(r)[:].rearrange("p (e t) -> p e t", e=2),
                                  xsT_h[:, e, :].bitcast(F32), ALU.subtract).then_inc(*prep_dve[ly].done(f"xs{r}"))

            def hidden(ly, b, e, w):
                dve.wait_ge(*exp_act[ly].at(f"h{e}{w}", b))
                k = slice(2 * w, 2 * w + 2)
                dve.scalar_tensor_tensor(out=hid_l[:, e % 2, k, :], in0=hb[w][:].rearrange("p (k t) -> p k t", k=2), scalar=0.0,
                                         in1=hid_h[:, e % 2, k, :].bitcast(F32), op0=ALU.max,
                                         op1=ALU.subtract).then_inc(*exp_dve[ly].done(f"h{e}{w}"))

            def phase1(i):
                for half in range(HALVES + 1):
                    if half % 2 == 1 and has(i - 1):
                        hidden(1, i - 1, half // 2, 1)
                    if half == 0 and isinstance(i, int) and i == 0:
                        attn_stats(0)
                        attn_norm(0)
                    if half == 0 and has(i - 2):
                        scan_inputs(i - 2, 7)
                    if half < 3 and has(i - 2):
                        scan_weigh(i - 2, 5 + half)
                    if half == 1 and has(i - 3):
                        fin_add(2, i - 3)
                    if half in GROUP_HALVES and has(i):
                        attn_qk(i, half - 1)
                    if half == V_HALF and has(i):
                        attn_v(i)
                    if half == 3 and has(i - 2):
                        scan_y(i - 2, 1)
                        scan_skip(i - 2)
                    if half == 6 and has(i - 2):
                        scan_add(i - 2)
                        prep_stats(2, i - 2)
                    if half == 7 and has(i - 2):
                        prep_norm(2, i - 2)
                    if half == 9 and has(i - 2):
                        prep_top(2, i - 2)
                    if half == 10 and has(i - 2):
                        prep_weights(2, i - 2)
                    if has(i):
                        for r in attn_rounds(half):
                            attn_max(i, r)
                    if half % 2 == 0 and half < HALVES and has(i - 1):
                        hidden(1, i - 1, half // 2, 0)
                    if half in PREP_ROUNDS and has(i - 2):
                        prep_low(2, i - 2, PREP_ROUNDS[half])
                    if half == HALVES and has(i):
                        attn_out(i)

            def phase2(i):
                for half in range(HALVES + 1):
                    if half % 2 == 1 and has(i - 2):
                        hidden(2, i - 2, half // 2, 1)
                    if half == 1:
                        if has(i - 1):
                            fin_add(1, i - 1)
                            scan_stats(i - 1)
                    if half == 2 and has(i - 1):
                        scan_norm(i - 1)
                    if half == 2 and has(i):
                        attn_add(i)
                        prep_stats(1, i)
                    if half == 3 and has(i):
                        prep_norm(1, i)
                    if half == 5 and has(i - 1):
                        scan_dpre(i - 1)
                    if half == 5 and has(i):
                        prep_top(1, i)
                    if half == 7 and has(i - 1):
                        scan_delta(i - 1)
                    if half == 7 and has(i):
                        prep_weights(1, i)
                    if 9 <= half < HALVES and has(i - 1):
                        scan_inputs(i - 1, half - 9)
                    if half in PREP_ROUNDS and has(i):
                        prep_low(1, i, PREP_ROUNDS[half])
                    if half == 14 and has(i + 1):
                        attn_stats(i + 1)
                    if half == HALVES and has(i + 1):
                        attn_norm(i + 1)
                    if 11 <= half < HALVES and has(i - 1):
                        scan_weigh(i - 1, half - 11)
                    if half == 15 and has(i - 1):
                        scan_y(i - 1, 0)
                    if half % 2 == 0 and half < HALVES and has(i - 2):
                        hidden(2, i - 2, half // 2, 0)

            run(dve, phase1, phase2)

        @block.tensor
        def _(pe):
            pe.wait_ge(c_pool, 6 + E + 3)
            pe.wait_ge(w_attn, W_ATTN)
            pe.wait_ge(w_scan, W_SCAN)
            pe.wait_ge(w_gate, 16)

            def transposes(dst, src, progress, event):
                for c in range(T):
                    last = pe.transpose(dst[:, c * P:(c + 1) * P], src[:, c, :], ident[:])
                last.then_inc(*progress.done(event))

            def token_products(dst, srcT, w, progress, event):
                for c in range(T):
                    last = pe.matmul(dst[:, c * P:(c + 1) * P], srcT[:, c * P:(c + 1) * P], w[:], start=True, stop=True)
                last.then_inc(*progress.done(event))

            def attn_xnT(b):
                wait_latest(pe, (prep_dve[1], f"xs{E // 2 - 1}", b - 1))
                pe.wait_ge(*attn_dve.at("xn", b))
                transposes(ma, a_xn, attn_pe, "xnT")

            def attn_qk(b, g):
                if g == 0:
                    pe.wait_ge(*attn_act.at("xnT", b))
                elif g == 1:
                    wait_latest(pe, (fin_dve[2], "x", b - 3), (prep_dve[1], f"xs{E // 2 - 2}", b - 1))
                else:
                    pe.wait_ge(*attn_dve.at(f"qk{g - 2}", b))
                for n in range(2):
                    last = pe.matmul(qk_bank(g)[:, n * L:(n + 1) * L], wqk_s[:, g, n, :], a_xnT[:], start=True, stop=True)
                last.then_inc(*attn_pe.done(f"qk{g}"))

            def attn_v(b):
                pe.wait_ge(*attn_dve.at(f"qk{HG - 2}", b))
                token_products(ma, a_xnT, wv_s, attn_pe, "v")

            def attn_score(b, r):
                g, j = r // HG, r % HG
                if j == 0:
                    pe.wait_ge(*attn_dve.at(f"qk{g}", b))
                if r >= NSC:
                    pe.wait_ge(*attn_act.at(f"exp{r - NSC}", b))
                else:
                    wait_latest(pe, (scan_dve, f"X{last_chunk[r]}", b - 2), (attn_act, f"exp{last_round[r]}", b - 1))
                rows = slice(32 * j, 32 * j + 3 * DH)
                for c in range(T):
                    last = pe.matmul(sc[r % NSC][:, c * L:(c + 1) * L], qk[rows, g, 0, c * P:(c + 1) * P], qk[rows, g, 1, :],
                                     start=True, stop=True)
                last.then_inc(*attn_pe.done(f"score{r}"))

            def attn_oT(b):
                wait_latest(pe, (prep_dve[2], f"xs{E // 2 - 1}", b - 2), (attn_dve, "v", b))
                pe.wait_ge(*attn_dve.at("o", b))
                transposes(ma, v_s, attn_pe, "oT")

            def attn_proj(b):
                wait_latest(pe, (fin_dve[1], "x", b - 1))
                pe.wait_ge(*attn_act.at("oT", b))
                token_products(mp, a_xnT, wo_s, attn_pe, "out")

            def scan_uT(b):
                wait_latest(pe, (attn_act, "oT", b + 1), (prep_dve[2], f"xs{E // 2 - 1}", b - 1))
                pe.wait_ge(*scan_dve.at("u", b))
                transposes(ma, u_s, scan_pe, "uT")

            def scan_xdbl(b):
                pe.wait_ge(*scan_act.at("uT", b))
                pe.matmul(ma[0:R, 0:L], wx_s[:, 0:R], uT[:], start=True, stop=True)
                for c in range(T):
                    o = L + c * 2 * N
                    last = pe.matmul(ma[:, o:o + 2 * N], uT[:, c * P:(c + 1) * P], wx_s[:, R:R + 2 * N], start=True, stop=True)
                last.then_inc(*scan_pe.done("xdbl"))

            def scan_dpre(b):
                pe.wait_ge(*scan_act.at("bc", b))
                token_products(ma, dlrT, wdt_s, scan_pe, "dpre")

            def scan_R(b):
                pe.wait_ge(*scan_dve.at("delta", b))
                pe.matmul(ma[:, 0:P], after[:], delta[:, 0, :], start=True, stop=False)
                pe.matmul(ma[:, 0:P], ones[:], delta[:, 1, :], start=False, stop=True)
                pe.matmul(ma[:, P:2 * P], after[:], delta[:, 1, :], start=True, stop=True).then_inc(*scan_pe.done("R"))

            def scan_sums(b, k):
                c, s, _ = quarter(k)
                pe.wait_ge(*scan_dve.at(f"P{k}", b))
                if k >= NSC:
                    pe.wait_ge(*scan_dve.at(f"X{k - NSC}", b))
                else:
                    wait_latest(pe, (attn_act, f"exp{last_round[k]}", b + 1), (scan_dve, f"X{last_chunk[k]}", b - 1))
                if c == 1:
                    pe.matmul(sc[k % NSC][:], ones[:], Pb[:, 0, s], start=True, stop=False)
                pe.matmul(sc[k % NSC][:], upto[:], Pb[:, c, s], start=(c == 0), stop=True).then_inc(*scan_pe.done(f"S{k}"))

            def scan_yT(b):
                wait_latest(pe, (attn_dve, f"qk{HG - 1}", b + 2), (fin_dve[2], "x", b - 1),
                            (prep_dve[1], f"xs{E // 2 - 2}", b + 1))
                pe.wait_ge(*scan_dve.at("yD", b))
                transposes(mp, y_s, scan_pe, "yT")

            def scan_proj(b):
                pe.wait_ge(*scan_act.at("yT", b))
                token_products(mp, uT, wout_s, scan_pe, "out")

            def prep_xnT(ly, b):
                pe.wait_ge(*prep_dve[ly].at("xn", b))
                transposes(mp, p_xn, prep_pe[ly], "xnT")

            def prep_logits(ly, b):
                pe.wait_ge(*prep_act[ly].at("xnT", b))
                for c in range(T):
                    last = pe.matmul(mp[:, L + c * E:L + (c + 1) * E], p_xnT[:, c * P:(c + 1) * P], gate_s[:], start=True, stop=True)
                last.then_inc(*prep_pe[ly].done("lg"))

            def prep_xsT(ly, b, r):
                if r == 0:
                    pe.wait_ge(*prep_dve[ly].at("lg", b))
                    pe.wait_ge(*prep_pool[ly].at("xs1", b))
                elif r == 1 and ly == 2:
                    wait_latest(pe, (attn_dve, "v", b + 2), (scan_act, "R", b))
                elif r == 1:
                    wait_latest(pe, (scan_act, "R", b - 1), (attn_act, "oT", b))
                else:
                    pe.wait_ge(*prep_dve[ly].at(f"xs{r - 2}", b))
                for e in range(2):
                    for c in range(T):
                        o = (e * T + c) * P
                        last = pe.transpose(round_bank(r)[:, o:o + P], xs[:, c, 2 * r + e, :], ident[:])
                last.then_inc(*prep_pe[ly].done(f"xs{r}"))

            def fin_t(ly, b):
                last_xs = f"xs{E // 2 - 2}"
                if ly == 2:
                    wait_latest(pe, (prep_dve[1], last_xs, b + 2), (fin_dve[1], "x", b + 1), (prep_dve[2], last_xs, b))
                else:
                    wait_latest(pe, (prep_dve[2], last_xs, b - 1), (prep_dve[1], last_xs, b))
                pe.wait_ge(*fin_act[ly].at("acc", b))
                for c in range(T):
                    last = pe.transpose(mp[:, c * P:(c + 1) * P], accT[:, c * P:(c + 1) * P], ident[:])
                last.then_inc(*fin_pe[ly].done("t"))

            def expert_up(ly, b, e):
                if e % 2 == 0:
                    pe.wait_ge(*prep_dve[ly].at(f"xs{e // 2}", b))
                for w in range(2):
                    if e:
                        pe.wait_ge(*exp_dve[ly].at(f"h{e - 1}{w}", b))
                    else:
                        wait_latest(pe, *((exp_dve[l], f"h{E - 1}{w}", n) for l, n in previous_pass(ly, b)))
                    for k in range(2):
                        f = slice(e * FF + (2 * w + k) * P, e * FF + (2 * w + k + 1) * P)
                        for wt, xt in ((w1_h, xsT_h), (w1_l, xsT_h), (w1_h, xsT_l)):
                            last = pe.matmul(hb[w][:, k * L:(k + 1) * L], wt[:, f], xt[:, e, :], start=(wt is w1_h and xt is xsT_h),
                                             stop=(xt is xsT_l))
                    last.then_inc(*exp_pe[ly].done(f"h{e}{w}"))

            def expert_down(ly, b, e):
                if e == 0:
                    wait_latest(pe, *((fin_act[l], "acc", n) for l, n in previous_pass(ly, b)))
                for ready, wt, ht in ((exp_act, w2_h, hid_h), (exp_act, w2_l, hid_h), (exp_dve, w2_h, hid_l)):
                    for k in range(FC):
                        if k % 2 == 0:
                            pe.wait_ge(*ready[ly].at(f"h{e}{k // 2}", b))
                        f = slice((e * FC + k) * P, (e * FC + k + 1) * P)
                        last = pe.matmul(acc[:, 0:L], wt[:, f], ht[:, e % 2, k, :], start=(e == 0 and k == 0 and ready is exp_act and wt is w2_h),
                                         stop=(e == E - 1 and k == FC - 1 and ht is hid_l))
                if e == E - 1:
                    last.then_inc(*exp_pe[ly].done("sum"))

            def experts(ly, b, half):
                if half % 2 == 0:
                    expert_up(ly, b, half // 2)
                elif half > 1:
                    expert_down(ly, b, half // 2 - 1)

            def phase1(i):
                if isinstance(i, int) and i == 1:
                    pe.wait_ge(c_dve, 8)
                for half in range(HALVES):
                    if half < 2 and has(i - 2):
                        scan_sums(i - 2, 6 + half)
                    if half == 1 and has(i - 3):
                        fin_t(2, i - 3)
                    if half == 0 and has(i):
                        attn_xnT(i)
                    if half in GROUP_HALVES and has(i):
                        attn_qk(i, half - 1)
                    if half == V_HALF and has(i):
                        attn_v(i)
                    if half == 5 and has(i - 2):
                        scan_yT(i - 2)
                    if half == 6 and has(i - 2):
                        scan_proj(i - 2)
                    if half == 8 and has(i - 2):
                        prep_xnT(2, i - 2)
                    if half == 9 and has(i - 2):
                        prep_logits(2, i - 2)
                    if half in PREP_ROUNDS and has(i - 2):
                        prep_xsT(2, i - 2, PREP_ROUNDS[half])
                    if has(i):
                        for r in attn_rounds(half):
                            attn_score(i, r)
                    if has(i - 1):
                        experts(1, i - 1, half)
                if has(i - 1):
                    expert_down(1, i - 1, E - 1)
                if has(i - 2):
                    prep_xsT(2, i - 2, E // 2 - 1)

            def phase2(i):
                for half in range(HALVES):
                    if half == 1 and has(i - 1):
                        fin_t(1, i - 1)
                    if half == 0 and has(i):
                        attn_oT(i)
                    if half == 2 and has(i):
                        attn_proj(i)
                    if half == 3 and has(i - 1):
                        scan_uT(i - 1)
                    if half == 4 and has(i - 1):
                        scan_xdbl(i - 1)
                    if half == 5 and has(i - 1):
                        scan_dpre(i - 1)
                    if half == 4 and has(i):
                        prep_xnT(1, i)
                    if half == 5 and has(i):
                        prep_logits(1, i)
                    if half == 8 and has(i - 1):
                        scan_R(i - 1)
                    if half in PREP_ROUNDS and has(i):
                        prep_xsT(1, i, PREP_ROUNDS[half])
                    if half >= 10 and has(i - 1):
                        scan_sums(i - 1, half - 10)
                    if has(i - 2):
                        experts(2, i - 2, half)
                if has(i - 2):
                    expert_down(2, i - 2, E - 1)
                if has(i):
                    prep_xsT(1, i, E // 2 - 1)

            run(pe, phase1, phase2)


_DRAM = ["x", "wqkT", "wvT", "b_qk", "b_v", "woT", "b_o", "W_x", "W_dt", "b_dt", "A_logT", "D", "W_out", "b_out",
         "gate_w", "w1", "w2"]


def kernel(**inputs):
    import numpy as _np
    import concourse.bacc as _bacc
    from concourse import mybir as _mybir
    from concourse.bass_utils import run_bass_kernel_spmd as _run

    a = {k: _np.asarray(v) for k, v in inputs.items()}
    D = a["L0_attn_a_x"].shape[-1]
    H = 16
    w_in = a["L0_attn_a_w_in"].reshape(H, 3, D // H, D)
    b_in = a["L0_attn_a_b_in"].reshape(H, 3, D // H)


    def head_rows(w):
        dh = D // H
        g = w.reshape(4, 4, 2, dh, w.shape[-1]).transpose(0, 2, 1, 3, 4)
        rows = _np.zeros(g.shape[:3] + (4 * dh, w.shape[-1]), w.dtype)
        for copy in range(3):
            rows[:, :, :, copy * dh:(copy + 1) * dh] = g
        return rows

    host = {
        "x": a["L0_attn_a_x"],
        "wqkT": head_rows(w_in[:, 0:2]).transpose(4, 0, 1, 2, 3).reshape(D, 4, 2, D),
        "wvT": w_in[:, 2].reshape(D, D).T,
        "b_qk": head_rows(b_in[:, 0:2, :, None])[..., 0].transpose(2, 3, 0, 1).reshape(D, 4, 2), "b_v": b_in[:, 2].reshape(D),
        "woT": a["L0_attn_a_w_out"].T, "b_o": a["L0_attn_a_b_out"],
        "W_x": a["L0_attn_b_W_x"], "W_dt": a["L0_attn_b_W_dt"], "b_dt": a["L0_attn_b_b_dt"],
        "A_logT": a["L0_attn_b_A_log"].T.reshape(-1), "D": a["L0_attn_b_D"],
        "W_out": a["L0_attn_b_W_out"], "b_out": a["L0_attn_b_b_out"],
        "gate_w": a["L0_ffn_gate_w"], "w1": a["L0_ffn_w1"], "w2": a["L0_ffn_w2"],
    }
    nc = _bacc.Bacc("TRN2", target_bir_lowering=False, num_devices=1)
    arrays, args = {}, []
    for name in _DRAM:
        v = _np.ascontiguousarray(host[name])
        arrays[f"in_{name}"] = v
        args.append(nc.dram_tensor(f"in_{name}", v.shape, _mybir.dt.from_np(v.dtype), kind="ExternalInput").ap())
    shape = a["L0_attn_a_x"].shape
    args.append(nc.dram_tensor("out_0", shape, F32, kind="ExternalOutput").ap())
    moe_hybrid_kernel(nc, *args)
    r = _run(nc, [arrays], core_ids=[0])
    return r.results[0]["out_0"]
```

```python
from contextlib import ExitStack

import concourse.bass as bass
from concourse import mybir

P = 128
F32 = mybir.dt.float32
F32R = mybir.dt.float32r
U32 = mybir.dt.uint32
ALU = mybir.AluOpType
ACT = mybir.ActivationFunctionType
AX = mybir.AxisListType

LN_EPS = 1e-5
SCAN_EPS = 1e-12


class Progress:

    def __init__(self, sem, events):
        self.sem, self.events, self.told = sem, events, 0

    def at(self, event, b):
        return self.sem, b * len(self.events) + (self.events.index(event) + 1)

    def done(self, event):
        assert self.events[self.told % len(self.events)] == event, (event, self.events[self.told % len(self.events)])
        self.told += 1
        return self.sem, 1


def moe_hybrid_kernel(nc, x, wqkT, wvT, b_qk, b_v, woT, b_o, W_x, W_dt, b_dt, A_logT, D_skip, W_out, b_out2,
                      gate_w, w1, w2, out):
    NSEQ, L, D = x.shape
    T = L // P
    H = 16
    DH = D // H
    E, _, FF = w1.shape
    FC = FF // P
    R = W_dt.shape[0]
    N = A_logT.shape[0] // D
    SCALE = float(DH) ** -0.5
    assert D == P and T == 2 and FC == 4 and E == 8 and N == 16
    HALVES = 2 * E
    NSC = 3
    ROUNDS = H
    HG = 4
    LOW_COPY = (2, 1)
    CHUNKS = T * N * D // 512

    x_v = x.rearrange("b (c p) d -> b p c d", p=P)
    out_v = out.rearrange("b (c p) d -> b p c d", p=P)

    ctx = ExitStack()
    with ctx:
        def sb(name, shape, dt=F32):
            return ctx.enter_context(nc.sbuf_tensor(name, shape, dt))

        def bank(name):
            return ctx.enter_context(nc.psum_tensor(name, [P, 512], F32))

        def sem(name):
            return ctx.enter_context(nc.semaphore(name))

        ident = sb("ident", [P, P])
        upto = sb("upto", [P, P])
        after = sb("after", [P, P])
        ones = sb("ones", [P, P])
        upto_r = sb("upto_r", [P, P], F32R)
        ones_r = sb("ones_r", [P, P], F32R)
        iota8 = sb("iota8", [P, E])
        tick = sb("tick", [P, 1])
        copy_rows = sb("copy_rows", [P, 4])
        ln_eps = sb("ln_eps", [P, 1])
        scan_eps = sb("scan_eps", [P, 1])
        wqk_s = sb("wqk_s", [P, HG, 2, P])
        wv_s = sb("wv_s", [P, P])
        bqk_s = sb("bqk_s", [P, HG, 2])
        bqk_m = sb("bqk_m", [P, HG, 2])
        bv_s = sb("bv_s", [P, P])
        wo_s = sb("wo_s", [P, P])
        bo_s = sb("bo_s", [P, P])
        wx_s = sb("wx_s", [P, R + 2 * N])
        wdt_s = sb("wdt_s", [R, P])
        bdt_s = sb("bdt_s", [P, P])
        Abc = sb("Abc", [P, N * D])
        D_s = sb("D_s", [P, P])
        wout_s = sb("wout_s", [P, P])
        bout_s = sb("bout_s", [P, P])
        gate_s = sb("gate_s", [P, E])
        w1_h = sb("w1_h", [P, E * FF], F32R)
        w1_l = sb("w1_l", [P, E * FF], F32R)
        w2_h = sb("w2_h", [P, E * FC * P], F32R)
        w2_l = sb("w2_l", [P, E * FC * P], F32R)

        xin = sb("xin", [P, T, P])
        x1 = sb("x1", [P, T, P])
        x2 = sb("x2", [P, T, P])
        x3 = sb("x3", [P, T, P])
        xo = sb("xo", [P, T, P])
        a_st = sb("a_st", [P, T, 6])
        a_mv = sb("a_mv", [P, T, 2])
        a_lv = sb("a_lv", [P, T])
        a_rs = sb("a_rs", [P, T])
        a_xn = sb("a_xn", [P, T, P])
        a_xnT = sb("a_xnT", [P, L])
        qk = sb("qk", [P, HG, 2, L], F32R)
        v_s = sb("v_s", [P, T, P])
        nmx = sb("nmx", [P, T, H])
        Z = sb("Z", [P, T, H])
        rz = sb("rz", [P, T, H])
        attsum = sb("attsum", [P, T, H])
        s_st = sb("s_st", [P, T, 6])
        s_mv = sb("s_mv", [P, T, 2])
        s_lv = sb("s_lv", [P, T])
        s_rs = sb("s_rs", [P, T])
        u_s = sb("u_s", [P, T, P])
        uT = sb("uT", [P, L])
        dlrT = sb("dlrT", [R, L])
        bc = sb("bc", [P, T, 2 * N])
        dneg = sb("dneg", [P, T, P])
        delta = sb("delta", [P, T, P])
        du = sb("du", [P, T, P])
        Rs = sb("Rs", [P, T, P])
        SLOTS, REC_SLOTS = 4, 6
        rings = sb("rings", [P, SLOTS + REC_SLOTS, 4 * D])
        P_h = sb("P_h", [P, T, N * D], F32R)
        P_l = sb("P_l", [P, T, N * D], F32R)
        ysum = sb("ysum", [P, 4 * D])
        y_s = sb("y_s", [P, T, P])
        uD = sb("uD", [P, T, P])
        p_st = sb("p_st", [P, T, 6])
        p_mv = sb("p_mv", [P, T, 2])
        p_lv = sb("p_lv", [P, T])
        p_rs = sb("p_rs", [P, T])
        p_xn = sb("p_xn", [P, T, P])
        lg = sb("lg", [P, T, E])
        top = sb("top", [P, T, 8])
        topi = sb("topi", [P, T, 8], U32)
        tdiff = sb("tdiff", [P, T, 2])
        texp = sb("texp", [P, T, 2])
        tsum = sb("tsum", [P, T])
        trec = sb("trec", [P, T])
        tw = sb("tw", [P, T, 2])
        hot = sb("hot", [P, T, 2, E])
        hotw = sb("hotw", [P, T, 2, E])
        comb = sb("comb", [P, T, E])
        xs = sb("xs", [P, T, E, P])
        xsT_h = sb("xsT_h", [P, E, L], F32R)
        xsT_l = sb("xsT_l", [P, E, L], F32R)
        accT = sb("accT", [P, L])
        hid_h = sb("hid_h", [P, 2, FC, L], F32R)
        hid_l = sb("hid_l", [P, 2, FC, L], F32R)

        hb = [bank("h_bank0"), bank("h_bank1")]
        acc = bank("acc_bank")
        sc = [bank(f"sc_bank{n}") for n in range(NSC)]
        ma = bank("mix_bank")
        mp = bank("prep_bank")

        w_attn, w_scan, w_gate = (sem(f"w_{n}") for n in ("attn", "scan", "gate"))
        w_loaded = [sem(f"w_loaded{e}") for e in range(E)]
        w_high, w_low = sem("w_high"), sem("w_low")
        c_pool, c_dve, c_act = sem("const_pool"), sem("const_dve"), sem("const_act")
        s_xin = sem("xin_loaded")
        s_out = sem("out_stored")

        rounds = range(ROUNDS)
        GROUP_HALVES = range(1, 1 + HG)
        V_HALF = 5
        ROUND_HALVES = range(3, 15)

        def attn_rounds(half):
            if half not in ROUND_HALVES:
                return range(0)
            n, k = len(ROUND_HALVES), half - ROUND_HALVES[0]
            return range(k * ROUNDS // n, (k + 1) * ROUNDS // n)

        def in_halves(group, v, score, later=0):
            events = []
            for half in range(HALVES + 1):
                if half in GROUP_HALVES:
                    events.append(f"{group}{half - 1}")
                if half == V_HALF and v:
                    events.append(v)
                events += [f"{score}{r}" for r in attn_rounds(half - later)]
            return events

        attn_dve = Progress(sem("attn_dve"), ["st0", "stats0", "stats1", "xn0", "xn"] + in_halves("qk", "v", "max")
                            + ["rz", "attsum", "o", "x1"])
        attn_act = Progress(sem("attn_act"), ["ln", "rstd", "xnT"] + in_halves("qk", None, "exp", 1) + ["oT"])
        attn_pe = Progress(sem("attn_pe"), ["xnT"] + in_halves("qk", "v", "score") + ["oT", "out"])
        attn_pool = Progress(sem("attn_pool"), ["xb"])

        chunks = range(CHUNKS)
        scan_dve = Progress(sem("scan_dve"), ["st0", "stats0", "stats1", "u0", "u", "dpre", "dneg", "delta", "du", "P0", "P1", "P2",
                                              "X0", "P3", "X1", "P4", "X2", "P5", "X3", "P6", "X4", "P7", "X5", "X6", "X7",
                                              "x3"])
        scan_act = Progress(sem("scan_act"), ["ln", "rstd", "uT", "dlr", "bc", "exp", "log", "R", "E0", "L0", "r0"]
                            + [e for k in range(1, CHUNKS) for e in (f"E{k}", f"L{k}", f"h{k - 1}", f"r{k}")] + [f"h{CHUNKS - 1}", "yT"])
        scan_pe = Progress(sem("scan_pe"), ["uT", "xdbl", "dpre", "R"] + [f"S{k}" for k in chunks] + ["yT", "out"])
        ORDER = ([("arg", 0), ("arg", 1), ("arg", 2)],
                 [("low", 0), ("arg", 3), ("low", 1), ("arg", 4), ("low", 2), ("arg", 5), ("arg", 6), ("low", 3), ("arg", 7),
                  ("add", 1), ("low", 4), ("add", 2), ("low", 5), ("add", 3)],
                 [("low", 6), ("low", 7), ("add", 5), ("add", 6), ("add", 7)])

        def order_events(order):
            return [e for w, k in order for e in [f"{w}{k}"] + ([f"half{k // 4}", f"y{k // 4}"] if w == "add" and k % 4 == 3 else [])]

        scan_pool = Progress(sem("scan_pool"), ["uD", "xb"] + order_events(ORDER[0] + ORDER[1] + ORDER[2]) + ["yD"])

        prep_dve, prep_act, prep_pe, prep_pool, exp_pe, exp_act, exp_dve, fin_pe, fin_act, fin_dve = ({} for _ in range(10))
        for ly in (1, 2):
            prep_dve[ly] = Progress(sem(f"prep{ly}_dve"), ["st0", "stats0", "stats1", "xn0", "xn", "lg", "top0", "top1", "topi",
                                                           "diff", "sum", "rec", "w", "hot", "hotw", "comb"] + (["scaled"] if ly == 1 else [])
                                    + [f"xs{r}" for r in range(E // 2)])
            prep_act[ly] = Progress(sem(f"prep{ly}_act"), ["ln", "rstd", "xnT", "texp"] + [f"xs{r}" for r in range(E // 2)])
            prep_pe[ly] = Progress(sem(f"prep{ly}_pe"), ["xnT", "lg"] + [f"xs{r}" for r in range(E // 2)])
            prep_pool[ly] = Progress(sem(f"prep{ly}_pool"), ["xs0"] + (["xs1"] if ly == 2 else []))
            exp_pe[ly] = Progress(sem(f"exp{ly}_pe"), [f"h{e}{w}" for e in range(E) for w in range(2)] + ["sum"])
            exp_act[ly] = Progress(sem(f"exp{ly}_act"), [f"h{e}{w}" for e in range(E) for w in range(2)])
            exp_dve[ly] = Progress(sem(f"exp{ly}_dve"), [f"h{e}{w}" for e in range(E) for w in range(2)])
            fin_pe[ly] = Progress(sem(f"fin{ly}_pe"), ["t"])
            fin_act[ly] = Progress(sem(f"fin{ly}_act"), ["acc"])
            fin_dve[ly] = Progress(sem(f"fin{ly}_dve"), ["x"])

        def has(b):
            return not isinstance(b, int) or 0 <= b < NSEQ

        def wait_latest(eng, *uses):
            for progress, event, b in uses:
                if has(b):
                    eng.wait_ge(*progress.at(event, b))
                    return

        def previous_pass(ly, b):
            return ((2, b - 2), (1, b - 1)) if ly == 1 else ((1, b + 1), (2, b - 1))

        PREP_ROUNDS = {13: 0, 14: 1, 15: 2, 16: 3}

        def run(eng, phase1, phase2):
            def step(i):
                phase1(i)
                phase2(i)
            for i in range(4):
                step(i)
            with eng.Fori(4, NSEQ - 1) as i:
                step(i)
            for i in range(NSEQ - 1, NSEQ + 3):
                step(i)

        last_round = [max(r for r in rounds if r % NSC == n) for n in range(NSC)]
        last_chunk = [max(k for k in chunks if k % NSC == n) for n in range(NSC)]

        def round_bank(r):
            return (mp, ma)[r % 2]

        def qk_bank(g):
            return (ma, mp)[g % 2]

        def exp_slot(k):
            return rings[:, k % SLOTS]

        def rec_slot(k):
            return rings[:, SLOTS + k % REC_SLOTS]

        def quarter(k):
            return k // 4, slice((k % 4) * 512, (k % 4 + 1) * 512), range((k % 4) * 4, (k % 4) * 4 + 4)

        block = ctx.enter_context(nc.Block())

        @block.sync
        def _(sp):
            def load_x(b):
                if not isinstance(b, int) or b > 0:
                    sp.wait_ge(*attn_dve.at("x1", b - 1))
                sp.dma_start(xin[:], x_v[b]).then_inc(s_xin, 16)

            def store(b):
                sp.wait_ge(*fin_dve[2].at("x", b))
                sp.dma_start(out_v[b], xo[:]).then_inc(s_out, 16)

            load_x(0)
            for dst, src in ((wqk_s, wqkT), (wv_s, wvT), (bqk_s, b_qk), (wo_s, woT)):
                sp.dma_start(dst[:], src).then_inc(w_attn, 16)
            for dst, src in ((bv_s, b_v), (bo_s, b_o)):
                sp.dma_start(dst[:], src.partition_broadcast(P)).then_inc(w_attn, 16)
            sp.dma_start(gate_s[:], gate_w).then_inc(w_gate, 16)
            for e in range(E):
                sp.dma_start(rings[:, e], w1[e]).then_inc(w_loaded[e], 16)
            for e in range(E):
                sp.wait_ge(w_low, e + 1)
                sp.dma_start(rings[:, e].rearrange("p (k d) -> p k d", k=FC),
                             w2[e].rearrange("(k f) d -> f k d", f=P)).then_inc(w_loaded[e], 16)

            def phase1(i):
                if has(i - 3):
                    store(i - 3)

            def phase2(i):
                if not isinstance(i, int) or i + 1 < NSEQ:
                    load_x(i + 1)

            for i in range(4):
                phase1(i)
                phase2(i)
            with sp.Fori(4, NSEQ - 1) as i:
                phase1(i)
                phase2(i)
            for i in range(NSEQ - 1, NSEQ + 3):
                phase1(i)
                phase2(i)
            sp.wait_ge(s_out, 16 * NSEQ)

        W_ATTN = 16 * 6
        W_SCAN = 16 * 7

        @block.gpsimd
        def _(pool):
            for dst, src in ((wx_s, W_x), (wdt_s, W_dt), (wout_s, W_out)):
                pool.dma_start(dst[:], src).then_inc(w_scan, 16)
            for dst, src in ((bdt_s, b_dt), (Abc, A_logT), (D_s, D_skip), (bout_s, b_out2)):
                pool.dma_start(dst[:], src.partition_broadcast(P)).then_inc(w_scan, 16)
            pool.memset(ident[:], 0.0).then_inc(c_pool, 1)
            pool.memset(upto[:], 1.0).then_inc(c_pool, 1)
            pool.memset(after[:], 1.0).then_inc(c_pool, 1)
            pool.memset(ones[:], 1.0).then_inc(c_pool, 1)
            for e in range(E):
                pool.memset(iota8[:, e:e + 1], float(e)).then_inc(c_pool, 1)
            pool.memset(ln_eps[:], LN_EPS).then_inc(c_pool, 1)
            pool.memset(scan_eps[:], SCAN_EPS).then_inc(c_pool, 1)
            pool.wait_ge(c_pool, 6 + E)
            pool.affine_select(out=ident[:], in_=ident[:], compare_op=ALU.not_equal, fill=1.0, base=0,
                               pattern=[[-1, P]], channel_multiplier=1).then_inc(c_pool, 1)
            pool.affine_select(out=upto[:], in_=upto[:], compare_op=ALU.is_ge, fill=0.0, base=0,
                               pattern=[[1, P]], channel_multiplier=-1).then_inc(c_pool, 1)
            pool.affine_select(out=after[:], in_=after[:], compare_op=ALU.is_gt, fill=0.0, base=0,
                               pattern=[[-1, P]], channel_multiplier=1).then_inc(c_pool, 1)
            pool.wait_ge(w_attn, W_ATTN)
            pool.wait_ge(w_scan, W_SCAN)

            def split(w, e):
                n, dst, high = ((0, w1_l, w1_h), (1, w2_l, w2_h))[w - 1]
                pool.wait_ge(w_high, n * E + e + 1)
                f = slice(e * FF, (e + 1) * FF)
                pool.tensor_tensor(dst[:, f], rings[:, e], high[:, f].bitcast(F32), ALU.subtract).then_inc(w_low, 1)

            def attn_residual(b):
                pool.wait_ge(s_xin, 16 * (b + 1))
                pool.wait_ge(*attn_dve.at("xn", b))
                pool.tensor_tensor(xin[:], xin[:], bo_s[:].unsqueeze(1).broadcast_to([P, T, P]),
                                   ALU.add).then_inc(*attn_pool.done("xb"))

            def scan_exponents(b, k):
                c, s, _ = quarter(k)
                if k == 0:
                    pool.wait_ge(*scan_act.at("R", b))
                if k < SLOTS:
                    wait_latest(pool, (scan_pool, f"low{k + SLOTS}", b - 1))
                else:
                    pool.wait_ge(*scan_pool.at(f"low{k - SLOTS}", b))
                pool.tensor_tensor(exp_slot(k).rearrange("p (n d) -> p n d", d=D), Rs[:, c].unsqueeze(1).broadcast_to([P, 4, D]),
                                   Abc[:, s].rearrange("p (n d) -> p n d", d=D), ALU.mult).then_inc(*scan_pool.done(f"arg{k}"))

            def scan_low(b, k):
                c, s, _ = quarter(k)
                pool.wait_ge(*scan_act.at(f"h{k}", b))
                pool.tensor_tensor(P_l[:, c, s], exp_slot(k), P_h[:, c, s].bitcast(F32), ALU.subtract).then_inc(*scan_pool.done(f"low{k}"))

            def scan_sum(b, k):
                c = k // 4
                pool.wait_ge(*scan_dve.at(f"X{k}", b))
                if k % 4 == 1:
                    if c:
                        pool.wait_ge(*scan_pool.at("y0", b))
                    else:
                        wait_latest(pool, (scan_pool, "y1", b - 1))
                    pool.tensor_tensor(ysum[:], rec_slot(k - 1), rec_slot(k), ALU.add).then_inc(*scan_pool.done(f"add{k}"))
                    return
                pool.wait_ge(*scan_pool.at(f"add{k - 1}", b))
                pool.tensor_tensor(ysum[:], ysum[:], rec_slot(k), ALU.add).then_inc(*scan_pool.done(f"add{k}"))
                if k % 4 == 3:
                    pool.wait_ge(*scan_pool.at(f"add{k}", b))
                    pool.tensor_tensor(ysum[:, 0:2 * D], ysum[:, 0:2 * D], ysum[:, 2 * D:4 * D],
                                       ALU.add).then_inc(*scan_pool.done(f"half{c}"))
                    pool.wait_ge(*scan_pool.at(f"half{c}", b))
                    wait_latest(pool, (scan_pe, "yT", b - 1))
                    pool.tensor_tensor(y_s[:, c], ysum[:, 0:D], ysum[:, D:2 * D], ALU.add).then_inc(*scan_pool.done(f"y{c}"))

            def scan_order(b, order):
                for what, k in order:
                    if what == "arg":
                        scan_exponents(b, k)
                    elif what == "low":
                        scan_low(b, k)
                    else:
                        scan_sum(b, k)

            def scan_rest(b):
                pool.wait_ge(*scan_dve.at("u", b))
                wait_latest(pool, (scan_pool, "yD", b - 1))
                pool.tensor_tensor(uD[:], u_s[:], D_s[:].unsqueeze(1).broadcast_to([P, T, P]),
                                   ALU.mult).then_inc(*scan_pool.done("uD"))
                pool.tensor_tensor(x2[:], x2[:], bout_s[:].unsqueeze(1).broadcast_to([P, T, P]),
                                   ALU.add).then_inc(*scan_pool.done("xb"))

            def scan_skip(b):
                pool.wait_ge(*scan_pool.at("y1", b))
                pool.tensor_tensor(y_s[:], y_s[:], uD[:], ALU.add).then_inc(*scan_pool.done("yD"))

            def prep_scale(ly, b, c):
                pool.wait_ge(*prep_dve[ly].at("comb", b))
                if c == 0:
                    if ly == 2:
                        wait_latest(pool, (prep_pe[1], f"xs{E // 2 - 1}", b + 1), (prep_pe[2], f"xs{E // 2 - 1}", b - 1))
                    else:
                        wait_latest(pool, (prep_pe[2], f"xs{E // 2 - 1}", b - 2), (prep_pe[1], f"xs{E // 2 - 1}", b - 1))
                pool.tensor_tensor(xs[:, c], p_xn[:, c].unsqueeze(1).broadcast_to([P, E, P]),
                                   comb[:, c].unsqueeze(2).broadcast_to([P, E, P]),
                                   ALU.mult).then_inc(*prep_pool[ly].done(f"xs{c}"))

            def phase1(i):
                if has(i - 2):
                    scan_order(i - 2, ORDER[2][:2])
                if has(i):
                    attn_residual(i)
                if has(i - 2):
                    scan_order(i - 2, ORDER[2][2:])
                    scan_skip(i - 2)
                    prep_scale(2, i - 2, 0)
                    prep_scale(2, i - 2, 1)
                if isinstance(i, int) and i == 0:
                    for e in range(E):
                        split(1, e)
                    pool.wait_ge(c_act, 1)
                    pool.tensor_scalar(Abc[:], Abc[:], -1.0, None, ALU.mult).then_inc(c_pool, 1)
                    pool.wait_ge(c_pool, 6 + E + 4)

            def phase2(i):
                if has(i - 1):
                    scan_rest(i - 1)
                    scan_order(i - 1, ORDER[0])
                if has(i):
                    prep_scale(1, i, 0)
                if isinstance(i, int) and i == 0:
                    for e in range(E):
                        split(2, e)
                if has(i - 1):
                    scan_order(i - 1, ORDER[1])

            run(pool, phase1, phase2)

        @block.scalar
        def _(act):
            act.preload_act_table_set("natural_log_exp_and_others")
            act.wait_ge(c_pool, 6 + E + 3)
            act.activation(upto_r[:], upto[:], ACT.Copy)
            act.activation(ones_r[:], ones[:], ACT.Copy)

            def split(w, e):
                n, dst = ((0, w1_h), (1, w2_h))[w - 1]
                act.wait_ge(w_loaded[e], 16 * (n + 1))
                act.activation(dst[:, e * FF:(e + 1) * FF], rings[:, e], ACT.Copy).then_inc(w_high, 1)

            def rstd(progress, dve, b, mv, lv, rs):
                act.wait_ge(*dve.at("stats1", b))
                act.activation(lv[:], mv[:, :, 1], ACT.Ln, bias=ln_eps[:]).then_inc(*progress.done("ln"))
                act.wait_ge(*progress.at("ln", b))
                act.activation(rs[:], lv[:], ACT.Exp, scale=-0.5).then_inc(*progress.done("rstd"))

            def attn_xnT(b):
                act.wait_ge(*attn_pe.at("xnT", b))
                act.activation(a_xnT[:], ma[:, 0:L], ACT.Copy).then_inc(*attn_act.done("xnT"))

            def attn_qk(b, g):
                act.wait_ge(*attn_pe.at(f"qk{g}", b))
                if g == 0:
                    act.wait_ge(c_dve, 5)
                for n in range(2):
                    last = act.activation(qk[:, g, n, :], qk_bank(g)[:, n * L:(n + 1) * L], ACT.Identity, bias=bqk_m[:, g, n:n + 1],
                                          scale=copy_rows[:, LOW_COPY[n]:LOW_COPY[n] + 1])
                last.then_inc(*attn_act.done(f"qk{g}"))

            def attn_exp(b, r):
                act.wait_ge(*attn_dve.at(f"max{r}", b))
                for c in range(T):
                    last = act.activation(sc[r % NSC][:, c * L:(c + 1) * L], sc[r % NSC][:, c * L:(c + 1) * L], ACT.Exp, bias=nmx[:, c, r:r + 1],
                                          accum_out=Z[:, c, r:r + 1])
                last.then_inc(*attn_act.done(f"exp{r}"))

            def attn_oT(b):
                act.wait_ge(*attn_pe.at("oT", b))
                act.activation(a_xnT[:], mp[:, 0:L], ACT.Copy).then_inc(*attn_act.done("oT"))

            def scan_uT(b):
                act.wait_ge(*scan_pe.at("uT", b))
                act.activation(uT[:], ma[:, 0:L], ACT.Copy).then_inc(*scan_act.done("uT"))

            def scan_xdbl(b):
                act.wait_ge(*scan_pe.at("xdbl", b))
                act.activation(dlrT[:], ma[0:R, 0:L], ACT.Copy).then_inc(*scan_act.done("dlr"))
                act.activation(bc[:], ma[:, L:L + T * 2 * N].rearrange("p (c n) -> p c n", c=T),
                               ACT.Copy).then_inc(*scan_act.done("bc"))

            def scan_softplus(b):
                act.wait_ge(*scan_dve.at("dneg", b))
                act.activation(dneg[:], dneg[:], ACT.Exp).then_inc(*scan_act.done("exp"))
                act.wait_ge(*scan_act.at("exp", b))
                act.activation(dneg[:], dneg[:], ACT.Ln, bias=ones[:, 0:1]).then_inc(*scan_act.done("log"))

            def scan_R(b):
                act.wait_ge(*scan_pe.at("R", b))
                act.activation(Rs[:], ma[:, 0:T * P].rearrange("p (c d) -> p c d", c=T),
                               ACT.Copy).then_inc(*scan_act.done("R"))

            def scan_E(b, k):
                act.wait_ge(*scan_pool.at(f"arg{k}", b))
                act.activation(exp_slot(k), exp_slot(k), ACT.Exp).then_inc(*scan_act.done(f"E{k}"))

            def scan_L(b, k):
                act.wait_ge(*scan_act.at(f"E{k}", b))
                if k >= REC_SLOTS:
                    last = k - REC_SLOTS
                    act.wait_ge(*scan_pool.at(f"add{last + (last % 4 == 0)}", b))
                elif k == 0:
                    wait_latest(act, (scan_pool, "y1", b - 1))
                act.activation(rec_slot(k), exp_slot(k), ACT.Ln, bias=scan_eps[:]).then_inc(*scan_act.done(f"L{k}"))

            def scan_r(b, k):
                act.wait_ge(*scan_act.at(f"L{k}", b))
                act.activation(rec_slot(k), rec_slot(k), ACT.Exp, scale=-1.0).then_inc(*scan_act.done(f"r{k}"))

            def scan_high(b, k):
                c, s, _ = quarter(k)
                act.wait_ge(*scan_dve.at(f"P{k}", b))
                if k == 0:
                    wait_latest(act, (scan_pe, f"S{CHUNKS - 1}", b - 1))
                act.activation(P_h[:, c, s], exp_slot(k), ACT.Copy).then_inc(*scan_act.done(f"h{k}"))

            def scan_exps(b, k):
                if k < CHUNKS:
                    scan_E(b, k)
                    scan_L(b, k)
                if k > 0:
                    scan_high(b, k - 1)
                if k < CHUNKS:
                    scan_r(b, k)

            def scan_yT(b):
                act.wait_ge(*scan_pe.at("yT", b))
                act.activation(uT[:], mp[:, 0:L], ACT.Copy).then_inc(*scan_act.done("yT"))

            def prep_xnT(ly, b):
                act.wait_ge(*prep_pe[ly].at("xnT", b))
                act.activation(accT[:], mp[:, 0:L], ACT.Copy).then_inc(*prep_act[ly].done("xnT"))

            def prep_texp(ly, b):
                act.wait_ge(*prep_dve[ly].at("diff", b))
                act.activation(texp[:], tdiff[:], ACT.Exp).then_inc(*prep_act[ly].done("texp"))

            def prep_xsT(ly, b, r):
                act.wait_ge(*prep_pe[ly].at(f"xs{r}", b))
                wait_latest(act, *((exp_pe[l], f"h{2 * r + 1}1", n) for l, n in previous_pass(ly, b)))
                act.activation(xsT_h[:, 2 * r:2 * r + 2, :], round_bank(r)[:].rearrange("p (e t) -> p e t", e=2),
                               ACT.Copy).then_inc(*prep_act[ly].done(f"xs{r}"))

            def fin_acc(ly, b):
                act.wait_ge(*exp_pe[ly].at("sum", b))
                act.activation(accT[:], acc[:, 0:L], ACT.Copy).then_inc(*fin_act[ly].done("acc"))

            def hidden(ly, b, e, w):
                act.wait_ge(*exp_pe[ly].at(f"h{e}{w}", b))
                act.activation(hid_h[:, e % 2, 2 * w:2 * w + 2, :], hb[w][:].rearrange("p (k t) -> p k t", k=2),
                               ACT.Relu).then_inc(*exp_act[ly].done(f"h{e}{w}"))

            def phase1(i):
                for half in range(HALVES + 1):
                    if half % 2 == 1 and has(i - 1):
                        hidden(1, i - 1, half // 2, 1)
                    if half == 0 and has(i - 3):
                        fin_acc(2, i - 3)
                    if half <= 1 and has(i - 2):
                        scan_exps(i - 2, 7 + half)
                    if half == 0 and has(i):
                        if isinstance(i, int) and i == 0:
                            rstd(attn_act, attn_dve, 0, a_mv, a_lv, a_rs)
                        attn_xnT(i)
                    if half in GROUP_HALVES and has(i):
                        attn_qk(i, half - 1)
                    if half == 5 and has(i - 2):
                        scan_yT(i - 2)
                    if half == 7 and has(i - 2):
                        rstd(prep_act[2], prep_dve[2], i - 2, p_mv, p_lv, p_rs)
                    if half == 8 and has(i - 2):
                        prep_xnT(2, i - 2)
                    if half == 10 and has(i - 2):
                        prep_texp(2, i - 2)
                    if half in PREP_ROUNDS and has(i - 2):
                        prep_xsT(2, i - 2, PREP_ROUNDS[half])
                    if has(i):
                        for r in attn_rounds(half - 1):
                            attn_exp(i, r)
                    if isinstance(i, int) and i == 0 and half < E:
                        split(1, half)
                    if half % 2 == 0 and half < HALVES and has(i - 1):
                        hidden(1, i - 1, half // 2, 0)

            def phase2(i):
                for half in range(HALVES + 1):
                    if isinstance(i, int) and i == 0:
                        if half == 0:
                            act.wait_ge(w_scan, W_SCAN)
                            act.activation(Abc[:], Abc[:], ACT.Exp).then_inc(c_act, 1)
                        if half >= HALVES - E and half < HALVES:
                            split(2, half - (HALVES - E))
                    if half % 2 == 1 and has(i - 2):
                        hidden(2, i - 2, half // 2, 1)
                    if half == 0 and has(i - 1):
                        fin_acc(1, i - 1)
                    if half == 2 and has(i - 1):
                        rstd(scan_act, scan_dve, i - 1, s_mv, s_lv, s_rs)
                    if half == 4 and has(i - 1):
                        scan_uT(i - 1)
                    if half == 3 and has(i):
                        attn_oT(i)
                    if half == 5 and has(i - 1):
                        scan_xdbl(i - 1)
                    if half == 5 and has(i):
                        rstd(prep_act[1], prep_dve[1], i, p_mv, p_lv, p_rs)
                    if half == 6 and has(i):
                        prep_xnT(1, i)
                    if half == 6 and has(i - 1):
                        scan_softplus(i - 1)
                    if half == 8 and has(i - 1):
                        scan_R(i - 1)
                    if half == 8 and has(i):
                        prep_texp(1, i)
                    if half in PREP_ROUNDS and has(i):
                        prep_xsT(1, i, PREP_ROUNDS[half])
                    if 9 <= half < HALVES and has(i - 1):
                        scan_exps(i - 1, half - 9)
                    if half == 7 and has(i + 1):
                        rstd(attn_act, attn_dve, i + 1, a_mv, a_lv, a_rs)
                    if half % 2 == 0 and half < HALVES and has(i - 2):
                        hidden(2, i - 2, half // 2, 0)

            run(act, phase1, phase2)

        @block.vector
        def _(dve):
            dve.wait_ge(c_pool, 6 + E + 3)
            dve.tensor_reduce(copy_rows[:], ident[:].rearrange("p (j r d) -> p r j d", j=HG, d=DH), AX.XY,
                              ALU.add).then_inc(c_dve, 1)
            dve.wait_ge(w_attn, W_ATTN)
            dve.tensor_scalar(wqk_s[:, :, 0, :], wqk_s[:, :, 0, :], SCALE, None, ALU.mult).then_inc(c_dve, 1)
            dve.tensor_scalar(bqk_s[:, :, 0], bqk_s[:, :, 0], SCALE, None, ALU.mult).then_inc(c_dve, 1)
            dve.wait_ge(c_dve, 3)
            for n in range(2):
                r = LOW_COPY[n]
                dve.tensor_scalar(bqk_m[:, :, n], bqk_s[:, :, n], copy_rows[:, r:r + 1], None, ALU.mult).then_inc(c_dve, 1)
            dve.wait_ge(w_scan, W_SCAN)

            def stats(progress, b, src, st, mv):
                dve.bn_stats(st[:, 0, :], src[:, 0, :])
                dve.bn_stats(st[:, 1, :], src[:, 1, :]).then_inc(*progress.done("st0"))
                dve.wait_ge(*progress.at("st0", b))
                dve.memset(tick[:], 0.0)
                dve.bn_aggr(mv[:, 0, :], st[:, 0, :]).then_inc(*progress.done("stats0"))
                dve.bn_aggr(mv[:, 1, :], st[:, 1, :]).then_inc(*progress.done("stats1"))

            def normalise(progress, act_progress, b, src, mv, rs, dst, events):
                dve.wait_ge(*act_progress.at("rstd", b))
                for c in range(T):
                    dve.tensor_scalar(dst[:, c, :], src[:, c, :], mv[:, c, 0:1], rs[:, c:c + 1], ALU.subtract,
                                      ALU.mult).then_inc(*progress.done(events[c]))

            def attn_stats(b):
                dve.wait_ge(s_xin, 16 * (b + 1))
                stats(attn_dve, b, xin, a_st, a_mv)

            def attn_norm(b):
                normalise(attn_dve, attn_act, b, xin, a_mv, a_rs, a_xn, ("xn0", "xn"))

            def attn_qk(b, g):
                dve.wait_ge(*attn_act.at(f"qk{g}", b))
                for n in range(2):
                    last = dve.scalar_tensor_tensor(out=qk[:, g, n, :], in0=qk_bank(g)[:, n * L:(n + 1) * L],
                                                    scalar=bqk_s[:, g, n:n + 1], in1=qk[:, g, n, :].bitcast(F32), op0=ALU.add,
                                                    op1=ALU.subtract)
                last.then_inc(*attn_dve.done(f"qk{g}"))

            def attn_v(b):
                dve.wait_ge(*attn_pe.at("v", b))
                dve.tensor_tensor(v_s[:], ma[:, 0:T * P].rearrange("p (c d) -> p c d", c=T),
                                  bv_s[:].unsqueeze(1).broadcast_to([P, T, P]), ALU.add).then_inc(*attn_dve.done("v"))

            def attn_max(b, r):
                dve.wait_ge(*attn_pe.at(f"score{r}", b))
                dve.tensor_reduce(nmx[:, :, r], sc[r % NSC][:].rearrange("p (c m) -> p c m", c=T), AX.X, ALU.max,
                                  negate=True).then_inc(*attn_dve.done(f"max{r}"))

            def attn_out(b):
                dve.wait_ge(*attn_act.at(f"exp{ROUNDS - 1}", b))
                dve.reciprocal(rz[:], Z[:]).then_inc(*attn_dve.done("rz"))
                dve.wait_ge(*attn_dve.at("rz", b))
                dve.tensor_tensor(attsum[:], Z[:], rz[:], ALU.mult).then_inc(*attn_dve.done("attsum"))
                dve.wait_ge(*attn_dve.at("attsum", b))
                dve.tensor_tensor(v_s[:].rearrange("p c (h d) -> p (c h) d", d=DH), v_s[:].rearrange("p c (h d) -> p (c h) d", d=DH),
                                  attsum[:].rearrange("p c h -> p (c h)").unsqueeze(2).broadcast_to([P, T * H, DH]),
                                  ALU.mult).then_inc(*attn_dve.done("o"))

            def attn_add(b):
                dve.wait_ge(*attn_pe.at("out", b))
                wait_latest(dve, (fin_dve[1], "x", b - 1))
                dve.wait_ge(*attn_pool.at("xb", b))
                dve.tensor_tensor(x1[:], mp[:, 0:T * P].rearrange("p (c d) -> p c d", c=T), xin[:],
                                  ALU.add).then_inc(*attn_dve.done("x1"))

            def scan_stats(b):
                dve.wait_ge(*fin_dve[1].at("x", b))
                stats(scan_dve, b, x2, s_st, s_mv)

            def scan_norm(b):
                normalise(scan_dve, scan_act, b, x2, s_mv, s_rs, u_s, ("u0", "u"))

            def scan_dpre(b):
                dve.wait_ge(*scan_pe.at("dpre", b))
                dve.tensor_tensor(delta[:], ma[:, 0:T * P].rearrange("p (c d) -> p c d", c=T),
                                  bdt_s[:].unsqueeze(1).broadcast_to([P, T, P]), ALU.add).then_inc(*scan_dve.done("dpre"))
                dve.wait_ge(*scan_dve.at("dpre", b))
                dve.scalar_tensor_tensor(out=dneg[:], in0=delta[:], scalar=-1.0, in1=delta[:], op0=ALU.mult,
                                         op1=ALU.min).then_inc(*scan_dve.done("dneg"))

            def scan_delta(b):
                dve.wait_ge(*scan_act.at("log", b))
                dve.scalar_tensor_tensor(out=delta[:], in0=delta[:], scalar=0.0, in1=dneg[:], op0=ALU.max,
                                         op1=ALU.add).then_inc(*scan_dve.done("delta"))
                dve.wait_ge(*scan_dve.at("delta", b))
                dve.tensor_tensor(du[:], delta[:], u_s[:], ALU.mult).then_inc(*scan_dve.done("du"))

            def scan_inputs(b, k):
                c, _, states = quarter(k)
                dve.wait_ge(*scan_act.at(f"L{k}", b))
                if k == 0:
                    dve.wait_ge(*scan_dve.at("du", b))
                for n in states:
                    e = exp_slot(k)[:, (n % 4) * D:(n % 4 + 1) * D]
                    last = dve.scalar_tensor_tensor(out=e, in0=e, scalar=bc[:, c, n:n + 1], in1=du[:, c, :], op0=ALU.mult, op1=ALU.mult)
                last.then_inc(*scan_dve.done(f"P{k}"))

            def scan_weigh(b, k):
                c, _, states = quarter(k)
                dve.wait_ge(*scan_pe.at(f"S{k}", b))
                dve.wait_ge(*scan_act.at(f"r{k}", b))
                for n in states:
                    s = slice((n % 4) * D, (n % 4 + 1) * D)
                    last = dve.scalar_tensor_tensor(out=rec_slot(k)[:, s], in0=sc[k % NSC][:, s], scalar=bc[:, c, N + n:N + n + 1],
                                                    in1=rec_slot(k)[:, s], op0=ALU.mult, op1=ALU.mult)
                last.then_inc(*scan_dve.done(f"X{k}"))

            def scan_add(b):
                dve.wait_ge(*scan_pe.at("out", b))
                wait_latest(dve, (fin_dve[2], "x", b - 1))
                dve.wait_ge(*scan_pool.at("xb", b))
                dve.tensor_tensor(x3[:], mp[:, 0:T * P].rearrange("p (c d) -> p c d", c=T), x2[:],
                                  ALU.add).then_inc(*scan_dve.done("x3"))

            def prep_stats(ly, b):
                src = x1 if ly == 1 else x3
                dve.wait_ge(*(attn_dve.at("x1", b) if ly == 1 else scan_dve.at("x3", b)))
                stats(prep_dve[ly], b, src, p_st, p_mv)

            def prep_norm(ly, b):
                src = x1 if ly == 1 else x3
                if ly == 2:
                    wait_latest(dve, (prep_pool[1], "xs0", b + 1), (prep_pool[2], "xs1", b - 1))
                else:
                    wait_latest(dve, (prep_pool[2], "xs1", b - 2), (prep_pool[1], "xs0", b - 1))
                normalise(prep_dve[ly], prep_act[ly], b, src, p_mv, p_rs, p_xn, ("xn0", "xn"))

            def prep_top(ly, b):
                pr = prep_dve[ly]
                dve.wait_ge(*prep_pe[ly].at("lg", b))
                dve.tensor_copy(lg[:], mp[:, L:L + T * E].rearrange("p (c e) -> p c e", c=T)).then_inc(*pr.done("lg"))
                dve.wait_ge(*pr.at("lg", b))
                dve.memset(tick[:], 0.0)
                dve.max(top[:, 0, :], lg[:, 0, :]).then_inc(*pr.done("top0"))
                dve.max(top[:, 1, :], lg[:, 1, :]).then_inc(*pr.done("top1"))
                dve.wait_ge(*pr.at("top1", b))
                dve.memset(tick[:], 0.0)
                dve.max_index(topi[:, 0, :], top[:, 0, :], lg[:, 0, :])
                dve.max_index(topi[:, 1, :], top[:, 1, :], lg[:, 1, :]).then_inc(*pr.done("topi"))
                dve.tensor_tensor(tdiff[:], top[:, :, 0:2], top[:, :, 0:1].broadcast_to([P, T, 2]),
                                  ALU.subtract).then_inc(*pr.done("diff"))

            def prep_weights(ly, b):
                pr = prep_dve[ly]
                dve.wait_ge(*prep_act[ly].at("texp", b))
                dve.tensor_reduce(tsum[:], texp[:], AX.X, ALU.add).then_inc(*pr.done("sum"))
                dve.wait_ge(*pr.at("sum", b))
                dve.reciprocal(trec[:], tsum[:]).then_inc(*pr.done("rec"))
                dve.wait_ge(*pr.at("rec", b))
                dve.tensor_tensor(tw[:], texp[:], trec[:].unsqueeze(2).broadcast_to([P, T, 2]), ALU.mult).then_inc(*pr.done("w"))
                for c in range(T):
                    last = dve.tensor_tensor(hot[:, c], topi[:, c, 0:2].unsqueeze(2).broadcast_to([P, 2, E]),
                                             iota8[:].unsqueeze(1).broadcast_to([P, 2, E]), ALU.is_equal)
                last.then_inc(*pr.done("hot"))
                dve.wait_ge(*pr.at("hot", b))
                dve.tensor_tensor(hotw[:].rearrange("p c k e -> p (c k) e"), hot[:].rearrange("p c k e -> p (c k) e"),
                                  tw[:].rearrange("p c k -> p (c k)").unsqueeze(2).broadcast_to([P, 2 * T, E]),
                                  ALU.mult).then_inc(*pr.done("hotw"))
                dve.wait_ge(*pr.at("hotw", b))
                dve.tensor_tensor(comb[:], hotw[:, :, 0, :], hotw[:, :, 1, :], ALU.add).then_inc(*pr.done("comb"))

            def prep_scale(b):
                dve.wait_ge(*prep_dve[1].at("comb", b))
                wait_latest(dve, (prep_pe[2], f"xs{E // 2 - 1}", b - 2), (prep_pe[1], f"xs{E // 2 - 1}", b - 1))
                dve.tensor_tensor(xs[:, 1], p_xn[:, 1].unsqueeze(1).broadcast_to([P, E, P]),
                                  comb[:, 1].unsqueeze(2).broadcast_to([P, E, P]), ALU.mult).then_inc(*prep_dve[1].done("scaled"))

            def fin_add(ly, b):
                dve.wait_ge(*fin_pe[ly].at("t", b))
                src, dst = (x1, x2) if ly == 1 else (x3, xo)
                if ly == 1:
                    wait_latest(dve, (scan_pool, "xb", b - 1))
                elif not isinstance(b, int) or b > 0:
                    dve.wait_ge(s_out, 16 * b)
                dve.tensor_tensor(dst[:], mp[:, 0:T * P].rearrange("p (c d) -> p c d", c=T), src[:],
                                  ALU.add).then_inc(*fin_dve[ly].done("x"))

            def prep_low(ly, b, r):
                dve.wait_ge(*prep_act[ly].at(f"xs{r}", b))
                e = slice(2 * r, 2 * r + 2)
                dve.tensor_tensor(xsT_l[:, e, :], round_bank(r)[:].rearrange("p (e t) -> p e t", e=2),
                                  xsT_h[:, e, :].bitcast(F32), ALU.subtract).then_inc(*prep_dve[ly].done(f"xs{r}"))

            def hidden(ly, b, e, w):
                dve.wait_ge(*exp_act[ly].at(f"h{e}{w}", b))
                k = slice(2 * w, 2 * w + 2)
                dve.scalar_tensor_tensor(out=hid_l[:, e % 2, k, :], in0=hb[w][:].rearrange("p (k t) -> p k t", k=2), scalar=0.0,
                                         in1=hid_h[:, e % 2, k, :].bitcast(F32), op0=ALU.max,
                                         op1=ALU.subtract).then_inc(*exp_dve[ly].done(f"h{e}{w}"))

            def phase1(i):
                for half in range(HALVES + 1):
                    if half % 2 == 1 and has(i - 1):
                        hidden(1, i - 1, half // 2, 1)
                    if half == 0 and isinstance(i, int) and i == 0:
                        attn_stats(0)
                        attn_norm(0)
                    if half == 1 and has(i - 3):
                        fin_add(2, i - 3)
                    if half < 4 and has(i - 2):
                        scan_weigh(i - 2, 4 + half)
                    if half == 0 and has(i - 2):
                        scan_inputs(i - 2, 7)
                    if half in GROUP_HALVES and has(i):
                        attn_qk(i, half - 1)
                    if half == V_HALF and has(i):
                        attn_v(i)
                    if half == 6 and has(i - 2):
                        scan_add(i - 2)
                        prep_stats(2, i - 2)
                    if half == 7 and has(i - 2):
                        prep_norm(2, i - 2)
                    if half == 9 and has(i - 2):
                        prep_top(2, i - 2)
                    if half == 10 and has(i - 2):
                        prep_weights(2, i - 2)
                    if has(i):
                        for r in attn_rounds(half):
                            attn_max(i, r)
                    if half % 2 == 0 and half < HALVES and has(i - 1):
                        hidden(1, i - 1, half // 2, 0)
                    if half in PREP_ROUNDS and has(i - 2):
                        prep_low(2, i - 2, PREP_ROUNDS[half])
                    if half == HALVES and has(i):
                        attn_out(i)

            def phase2(i):
                for half in range(HALVES + 1):
                    if half % 2 == 1 and has(i - 2):
                        hidden(2, i - 2, half // 2, 1)
                    if half == 1:
                        if has(i - 1):
                            fin_add(1, i - 1)
                            scan_stats(i - 1)
                    if half == 2 and has(i - 1):
                        scan_norm(i - 1)
                    if half == 4 and has(i):
                        attn_add(i)
                        prep_stats(1, i)
                    if half == 5 and has(i):
                        prep_norm(1, i)
                    if half == 6 and has(i - 1):
                        scan_dpre(i - 1)
                    if half == 7 and has(i):
                        prep_top(1, i)
                    if half == 7 and has(i + 1):
                        attn_norm(i + 1)
                    if half == 8 and has(i):
                        prep_weights(1, i)
                    if 12 <= half < HALVES and has(i - 1):
                        scan_weigh(i - 1, half - 12)
                    if 9 <= half < HALVES and has(i - 1):
                        scan_inputs(i - 1, half - 9)
                    if half in PREP_ROUNDS and has(i):
                        prep_low(1, i, PREP_ROUNDS[half])
                    if half == 6 and has(i - 1):
                        scan_delta(i - 1)
                    if half % 2 == 0 and half < HALVES and has(i - 2):
                        hidden(2, i - 2, half // 2, 0)
                    if half == 8 and has(i):
                        prep_scale(i)
                    if half == 5 and has(i + 1):
                        attn_stats(i + 1)

            run(dve, phase1, phase2)

        @block.tensor
        def _(pe):
            pe.wait_ge(c_pool, 6 + E + 3)
            pe.wait_ge(w_attn, W_ATTN)
            pe.wait_ge(c_dve, 5)
            pe.wait_ge(w_scan, W_SCAN)
            pe.wait_ge(w_gate, 16)

            def transposes(dst, src, progress, event):
                for c in range(T):
                    last = pe.transpose(dst[:, c * P:(c + 1) * P], src[:, c, :], ident[:])
                last.then_inc(*progress.done(event))

            def token_products(dst, srcT, w, progress, event):
                for c in range(T):
                    last = pe.matmul(dst[:, c * P:(c + 1) * P], srcT[:, c * P:(c + 1) * P], w[:], start=True, stop=True)
                last.then_inc(*progress.done(event))

            def attn_xnT(b):
                wait_latest(pe, (prep_dve[1], f"xs{E // 2 - 1}", b - 1))
                pe.wait_ge(*attn_dve.at("xn", b))
                transposes(ma, a_xn, attn_pe, "xnT")

            def attn_qk(b, g):
                if g == 0:
                    pe.wait_ge(*attn_act.at("xnT", b))
                elif g == 1:
                    wait_latest(pe, (fin_dve[2], "x", b - 3), (prep_dve[1], f"xs{E // 2 - 2}", b - 1))
                else:
                    pe.wait_ge(*attn_dve.at(f"qk{g - 2}", b))
                for n in range(2):
                    last = pe.matmul(qk_bank(g)[:, n * L:(n + 1) * L], wqk_s[:, g, n, :], a_xnT[:], start=True, stop=True)
                last.then_inc(*attn_pe.done(f"qk{g}"))

            def attn_v(b):
                pe.wait_ge(*attn_dve.at(f"qk{HG - 2}", b))
                token_products(ma, a_xnT, wv_s, attn_pe, "v")

            def attn_score(b, r):
                g, j = r // HG, r % HG
                if j == 0:
                    pe.wait_ge(*attn_dve.at(f"qk{g}", b))
                if r >= NSC:
                    pe.wait_ge(*attn_act.at(f"exp{r - NSC}", b))
                else:
                    wait_latest(pe, (scan_dve, f"X{last_chunk[r]}", b - 2), (attn_act, f"exp{last_round[r]}", b - 1))
                rows = slice(32 * j, 32 * j + 3 * DH)
                for c in range(T):
                    last = pe.matmul(sc[r % NSC][:, c * L:(c + 1) * L], qk[rows, g, 0, c * P:(c + 1) * P], qk[rows, g, 1, :],
                                     start=True, stop=True)
                last.then_inc(*attn_pe.done(f"score{r}"))

            def attn_oT(b):
                wait_latest(pe, (fin_dve[1], "x", b - 1))
                pe.wait_ge(*attn_dve.at("o", b))
                transposes(mp, v_s, attn_pe, "oT")

            def attn_proj(b):
                pe.wait_ge(*attn_act.at("oT", b))
                token_products(mp, a_xnT, wo_s, attn_pe, "out")

            def scan_uT(b):
                wait_latest(pe, (prep_dve[2], f"xs{E // 2 - 1}", b - 1), (attn_dve, "v", b + 1))
                pe.wait_ge(*scan_dve.at("u", b))
                transposes(ma, u_s, scan_pe, "uT")

            def scan_xdbl(b):
                pe.wait_ge(*scan_act.at("uT", b))
                pe.matmul(ma[0:R, 0:L], wx_s[:, 0:R], uT[:], start=True, stop=True)
                for c in range(T):
                    o = L + c * 2 * N
                    last = pe.matmul(ma[:, o:o + 2 * N], uT[:, c * P:(c + 1) * P], wx_s[:, R:R + 2 * N], start=True, stop=True)
                last.then_inc(*scan_pe.done("xdbl"))

            def scan_dpre(b):
                pe.wait_ge(*scan_act.at("bc", b))
                token_products(ma, dlrT, wdt_s, scan_pe, "dpre")

            def scan_R(b):
                pe.wait_ge(*scan_dve.at("delta", b))
                pe.matmul(ma[:, 0:P], after[:], delta[:, 0, :], start=True, stop=False)
                pe.matmul(ma[:, 0:P], ones[:], delta[:, 1, :], start=False, stop=True)
                pe.matmul(ma[:, P:2 * P], after[:], delta[:, 1, :], start=True, stop=True).then_inc(*scan_pe.done("R"))

            def scan_sums(b, k):
                c, s, _ = quarter(k)
                pe.wait_ge(*scan_pool.at(f"low{k}", b))
                if k >= NSC:
                    pe.wait_ge(*scan_dve.at(f"X{k - NSC}", b))
                else:
                    wait_latest(pe, (attn_act, f"exp{last_round[k]}", b + 1), (scan_dve, f"X{last_chunk[k]}", b - 1))
                products = [(upto_r, P_h[:, c, s]), (upto_r, P_l[:, c, s])]
                if c == 1:
                    products += [(ones_r, P_h[:, 0, s]), (ones_r, P_l[:, 0, s])]
                for n, (w, v) in enumerate(products):
                    last = pe.matmul(sc[k % NSC][:], w[:], v, start=(n == 0), stop=(n == len(products) - 1))
                last.then_inc(*scan_pe.done(f"S{k}"))

            def scan_yT(b):
                wait_latest(pe, (attn_dve, f"qk{HG - 1}", b + 2), (fin_dve[2], "x", b - 1),
                            (prep_dve[1], f"xs{E // 2 - 2}", b + 1))
                pe.wait_ge(*scan_pool.at("yD", b))
                transposes(mp, y_s, scan_pe, "yT")

            def scan_proj(b):
                pe.wait_ge(*scan_act.at("yT", b))
                token_products(mp, uT, wout_s, scan_pe, "out")

            def prep_xnT(ly, b):
                pe.wait_ge(*prep_dve[ly].at("xn", b))
                transposes(mp, p_xn, prep_pe[ly], "xnT")

            def prep_logits(ly, b):
                pe.wait_ge(*prep_act[ly].at("xnT", b))
                for c in range(T):
                    last = pe.matmul(mp[:, L + c * E:L + (c + 1) * E], accT[:, c * P:(c + 1) * P], gate_s[:], start=True, stop=True)
                last.then_inc(*prep_pe[ly].done("lg"))

            def prep_xsT(ly, b, r):
                if r == 0:
                    pe.wait_ge(*prep_dve[ly].at("lg", b))
                    if ly == 1:
                        pe.wait_ge(*prep_dve[ly].at("scaled", b))
                    pe.wait_ge(*prep_pool[ly].at("xs0" if ly == 1 else "xs1", b))
                elif r == 1 and ly == 2:
                    wait_latest(pe, (attn_dve, "v", b + 2), (scan_act, "R", b))
                elif r == 1:
                    wait_latest(pe, (scan_act, "R", b - 1), (attn_dve, "v", b))
                else:
                    pe.wait_ge(*prep_dve[ly].at(f"xs{r - 2}", b))
                for e in range(2):
                    for c in range(T):
                        o = (e * T + c) * P
                        last = pe.transpose(round_bank(r)[:, o:o + P], xs[:, c, 2 * r + e, :], ident[:])
                last.then_inc(*prep_pe[ly].done(f"xs{r}"))

            def fin_t(ly, b):
                last_xs = f"xs{E // 2 - 2}"
                if ly == 2:
                    wait_latest(pe, (prep_dve[1], last_xs, b + 2), (fin_dve[1], "x", b + 1), (prep_dve[2], last_xs, b))
                else:
                    wait_latest(pe, (prep_dve[2], last_xs, b - 1), (prep_dve[1], last_xs, b))
                pe.wait_ge(*fin_act[ly].at("acc", b))
                for c in range(T):
                    last = pe.transpose(mp[:, c * P:(c + 1) * P], accT[:, c * P:(c + 1) * P], ident[:])
                last.then_inc(*fin_pe[ly].done("t"))

            def expert_up(ly, b, e):
                if ly == 1 and isinstance(b, int) and b == 0:
                    pe.wait_ge(w_low, e + 1)
                if e % 2 == 0:
                    pe.wait_ge(*prep_dve[ly].at(f"xs{e // 2}", b))
                for w in range(2):
                    if e:
                        pe.wait_ge(*exp_dve[ly].at(f"h{e - 1}{w}", b))
                    else:
                        wait_latest(pe, *((exp_dve[l], f"h{E - 1}{w}", n) for l, n in previous_pass(ly, b)))
                    for k in range(2):
                        f = slice(e * FF + (2 * w + k) * P, e * FF + (2 * w + k + 1) * P)
                        for wt, xt in ((w1_h, xsT_h), (w1_l, xsT_h), (w1_h, xsT_l)):
                            last = pe.matmul(hb[w][:, k * L:(k + 1) * L], wt[:, f], xt[:, e, :], start=(wt is w1_h and xt is xsT_h),
                                             stop=(xt is xsT_l))
                    last.then_inc(*exp_pe[ly].done(f"h{e}{w}"))

            def expert_down(ly, b, e):
                if ly == 1 and isinstance(b, int) and b == 0:
                    pe.wait_ge(w_low, E + e + 1)
                if e == 0:
                    wait_latest(pe, *((fin_act[l], "acc", n) for l, n in previous_pass(ly, b)))
                for ready, wt, ht in ((exp_act, w2_h, hid_h), (exp_act, w2_l, hid_h), (exp_dve, w2_h, hid_l)):
                    for k in range(FC):
                        if k % 2 == 0:
                            pe.wait_ge(*ready[ly].at(f"h{e}{k // 2}", b))
                        f = slice((e * FC + k) * P, (e * FC + k + 1) * P)
                        last = pe.matmul(acc[:, 0:L], wt[:, f], ht[:, e % 2, k, :], start=(e == 0 and k == 0 and ready is exp_act and wt is w2_h),
                                         stop=(e == E - 1 and k == FC - 1 and ht is hid_l))
                if e == E - 1:
                    last.then_inc(*exp_pe[ly].done("sum"))

            def experts(ly, b, half):
                if half % 2 == 0:
                    expert_up(ly, b, half // 2)
                elif half > 1:
                    expert_down(ly, b, half // 2 - 1)

            def phase1(i):
                for half in range(HALVES):
                    if half == 1 and has(i - 3):
                        fin_t(2, i - 3)
                    if half == 0 and has(i):
                        attn_xnT(i)
                    if half in GROUP_HALVES and has(i):
                        attn_qk(i, half - 1)
                    if half == V_HALF and has(i):
                        attn_v(i)
                    if half == 5 and has(i - 2):
                        scan_yT(i - 2)
                    if half == 6 and has(i - 2):
                        scan_proj(i - 2)
                    if half == 8 and has(i - 2):
                        prep_xnT(2, i - 2)
                    if half == 9 and has(i - 2):
                        prep_logits(2, i - 2)
                    if half in PREP_ROUNDS and has(i - 2):
                        prep_xsT(2, i - 2, PREP_ROUNDS[half])
                    if has(i):
                        for r in attn_rounds(half):
                            attn_score(i, r)
                    if has(i - 1):
                        experts(1, i - 1, half)
                    if half < 3 and has(i - 2):
                        scan_sums(i - 2, 5 + half)
                    if half == HALVES - 1 and has(i - 2):
                        prep_xsT(2, i - 2, E // 2 - 1)
                if has(i - 1):
                    expert_down(1, i - 1, E - 1)

            def phase2(i):
                for half in range(HALVES):
                    if half == 1 and has(i - 1):
                        fin_t(1, i - 1)
                    if half == 4 and has(i):
                        attn_proj(i)
                    if half == 6 and has(i):
                        prep_xnT(1, i)
                    if half == 7 and has(i):
                        prep_logits(1, i)
                    if half in PREP_ROUNDS and has(i):
                        prep_xsT(1, i, PREP_ROUNDS[half])
                    if has(i - 2):
                        experts(2, i - 2, half)
                    if half == 3 and has(i - 1):
                        scan_uT(i - 1)
                    if half == 4 and has(i - 1):
                        scan_xdbl(i - 1)
                    if half == 5 and has(i - 1):
                        scan_dpre(i - 1)
                    if half >= 11 and has(i - 1):
                        scan_sums(i - 1, half - 11)
                    if half == HALVES - 1 and has(i):
                        prep_xsT(1, i, E // 2 - 1)
                    if half == 2 and has(i):
                        attn_oT(i)
                    if half == 7 and has(i - 1):
                        scan_R(i - 1)
                if has(i - 2):
                    expert_down(2, i - 2, E - 1)

            run(pe, phase1, phase2)


_DRAM = ["x", "wqkT", "wvT", "b_qk", "b_v", "woT", "b_o", "W_x", "W_dt", "b_dt", "A_logT", "D", "W_out", "b_out",
         "gate_w", "w1", "w2"]


def kernel(**inputs):
    import numpy as _np
    import concourse.bacc as _bacc
    from concourse import mybir as _mybir
    from concourse.bass_utils import run_bass_kernel_spmd as _run

    a = {k: _np.asarray(v) for k, v in inputs.items()}
    D = a["L0_attn_a_x"].shape[-1]
    H = 16
    w_in = a["L0_attn_a_w_in"].reshape(H, 3, D // H, D)
    b_in = a["L0_attn_a_b_in"].reshape(H, 3, D // H)


    def head_rows(w):
        dh = D // H
        g = w.reshape(4, 4, 2, dh, w.shape[-1]).transpose(0, 2, 1, 3, 4)
        rows = _np.zeros(g.shape[:3] + (4 * dh, w.shape[-1]), w.dtype)
        for copy in range(3):
            rows[:, :, :, copy * dh:(copy + 1) * dh] = g
        return rows

    host = {
        "x": a["L0_attn_a_x"],
        "wqkT": head_rows(w_in[:, 0:2]).transpose(4, 0, 1, 2, 3).reshape(D, 4, 2, D),
        "wvT": w_in[:, 2].reshape(D, D).T,
        "b_qk": head_rows(b_in[:, 0:2, :, None])[..., 0].transpose(2, 3, 0, 1).reshape(D, 4, 2), "b_v": b_in[:, 2].reshape(D),
        "woT": a["L0_attn_a_w_out"].T, "b_o": a["L0_attn_a_b_out"],
        "W_x": a["L0_attn_b_W_x"], "W_dt": a["L0_attn_b_W_dt"], "b_dt": a["L0_attn_b_b_dt"],
        "A_logT": a["L0_attn_b_A_log"].T.reshape(-1), "D": a["L0_attn_b_D"],
        "W_out": a["L0_attn_b_W_out"], "b_out": a["L0_attn_b_b_out"],
        "gate_w": a["L0_ffn_gate_w"], "w1": a["L0_ffn_w1"], "w2": a["L0_ffn_w2"],
    }
    nc = _bacc.Bacc("TRN2", target_bir_lowering=False, num_devices=1)
    arrays, args = {}, []
    for name in _DRAM:
        v = _np.ascontiguousarray(host[name])
        arrays[f"in_{name}"] = v
        args.append(nc.dram_tensor(f"in_{name}", v.shape, _mybir.dt.from_np(v.dtype), kind="ExternalInput").ap())
    shape = a["L0_attn_a_x"].shape
    args.append(nc.dram_tensor("out_0", shape, F32, kind="ExternalOutput").ap())
    moe_hybrid_kernel(nc, *args)
    r = _run(nc, [arrays], core_ids=[0])
    return r.results[0]["out_0"]
```
